# Optimizing a Trainium2 kernel written in Bass

```python
import numpy as np
import jax
import jax.numpy as jnp

def _softmax(x, axis=-1):
    return jax.nn.softmax(x, axis=axis)

def _gelu(x):
    return jax.nn.gelu(x, approximate=True)

def _silu(x):
    return jax.nn.silu(x)

def _sigmoid(x):
    return jax.nn.sigmoid(x)

def _layernorm(x, axis=-1, eps=1e-05):
    m = jnp.mean(x, axis=axis, keepdims=True)
    v = jnp.var(x, axis=axis, keepdims=True)
    return (x - m) / jnp.sqrt(v + eps)

def _scatter_add(tgt, idx, src, axis=0):
    return tgt.at[idx].add(src)

def _segment_sum(src, seg, n):
    return jax.ops.segment_sum(src, seg, n)
kernel_name = 'mk_gnn_resnorm_d4_gnn_r16_16accc'

def setup_inputs(seed: int=0):
    np.random.seed(seed)
    _w = jnp.asarray

    def _rec_inputs():
        import jax
        import jax.numpy as jnp
        _gk = jax.random.key(seed)
        x = -0.0003713 + 1 * jax.random.normal(jax.random.fold_in(_gk, 1), (6250, 128), jnp.float32)
        src = jax.random.randint(jax.random.fold_in(_gk, 2), (200000,), 0, 6250, jnp.int32)
        dst = jnp.minimum((6250 * jax.random.uniform(jax.random.fold_in(_gk, 3), (200000,)) ** 2.0).astype(jnp.int32), 99999)
        _o = jnp.argsort(dst, stable=True)
        src = src[_o]
        dst = dst[_o]
        edge_type_2 = jax.random.randint(jax.random.fold_in(_gk, 13), (200000,), 0, 2, jnp.int32)
        edge_type_64 = jax.random.randint(jax.random.fold_in(_gk, 14), (200000,), 0, 64, jnp.int32)
        edge_weight = jax.random.uniform(jax.random.fold_in(_gk, 15), (200000,), jnp.float32, 0.0, 1)
        return (x, src, dst, edge_type_2, edge_type_64, edge_weight)
    x, src, dst, edge_type_2, edge_type_64, edge_weight = _rec_inputs()

    def _L0_gnn_setup():
        import jax, jax.numpy as jnp
        import numpy as np
        N_NODES = 6250
        N_EDGES = 37500
        HIDDEN = 128
        NUM_REL = 64
        key = jax.random.key(seed)
        ks = jax.random.split(key, 8)
        node_states = jax.random.normal(ks[0], (N_NODES, HIDDEN), dtype=jnp.float32)
        edge_index = jax.random.randint(ks[1], (2, N_EDGES), 0, N_NODES, dtype=jnp.int64)
        edge_type_ids = jax.random.randint(ks[2], (N_EDGES,), 0, NUM_REL, dtype=jnp.int64)
        s = 1.0 / np.sqrt(HIDDEN)
        W_self = jax.random.uniform(ks[3], (HIDDEN, HIDDEN), jnp.float32, -s, s)
        b_self = jax.random.uniform(ks[4], (HIDDEN,), jnp.float32, -s, s)
        W_msg = jax.random.uniform(ks[5], (HIDDEN, HIDDEN), jnp.float32, -s, s)
        b_msg = jax.random.uniform(ks[6], (HIDDEN,), jnp.float32, -s, s)
        rel_emb = jax.random.normal(ks[7], (NUM_REL, HIDDEN), dtype=jnp.float32)
        return {'node_states': node_states, 'edge_index': edge_index, 'edge_type_ids': edge_type_ids, 'W_self': W_self, 'b_self': b_self, 'W_msg': W_msg, 'b_msg': b_msg, 'rel_emb': rel_emb}
    _L0_gnn_all = _L0_gnn_setup()
    _L0_gnn_in = {k: v for k, v in _L0_gnn_all.items() if k in ('W_self', 'b_self', 'W_msg', 'b_msg', 'rel_emb')}
    del _L0_gnn_all

    def _L1_gnn_setup():
        import jax, jax.numpy as jnp
        import numpy as np
        N = 6250
        E = 100000
        DIN = 128
        DOUT = 128
        H = 4
        DS = DOUT // H

        def _lrelu(x):
            return jnp.where(x > 0, x, 0.2 * x)
        key = jax.random.key(seed)
        ks = jax.random.split(key, 8)
        feat_in = jax.random.normal(ks[0], (N, DIN), dtype=jnp.float32)
        edge_row = jnp.sort(jax.random.randint(ks[1], (E,), 0, N, dtype=jnp.int32))
        edge_col = jax.random.randint(ks[2], (E,), 0, N, dtype=jnp.int32)
        edge_val = jnp.ones((E,), dtype=jnp.float32)
        lim = 1.0 / np.sqrt(DIN)
        W0 = jax.random.uniform(ks[3], (DOUT, DIN), minval=-lim, maxval=lim, dtype=jnp.float32)
        b0 = jnp.zeros((DOUT,), dtype=jnp.float32)
        W1 = jax.random.uniform(ks[4], (DOUT, DIN), minval=-lim, maxval=lim, dtype=jnp.float32)
        b1 = jnp.zeros((DOUT,), dtype=jnp.float32)
        glim = np.sqrt(6.0 / (2 * H * DS))
        attention = jax.random.uniform(ks[5], (2, H, DS), minval=-glim, maxval=glim, dtype=jnp.float32)
        scale = jnp.ones((2, H, DS), dtype=jnp.float32)
        offset = jnp.zeros((2, H, DS), dtype=jnp.float32)
        return {'feat_in': feat_in, 'edge_row': edge_row, 'edge_col': edge_col, 'edge_val': edge_val, 'W0': W0, 'b0': b0, 'W1': W1, 'b1': b1, 'attention': attention, 'scale': scale, 'offset': offset}
    _L1_gnn_all = _L1_gnn_setup()
    _L1_gnn_in = {k: v for k, v in _L1_gnn_all.items() if k in ('W0', 'b0', 'W1', 'b1', 'attention', 'scale', 'offset')}
    del _L1_gnn_all

    def _L2_gnn_setup():
        import jax, jax.numpy as jnp
        import numpy as np
        IN_DIM = 128
        OUT_DIM = 128
        N_NODES = 625
        N_EDGES = 40000
        key = jax.random.key(seed)
        ks = jax.random.split(key, 9)
        X = jax.random.normal(ks[0], (N_NODES, IN_DIM), dtype=jnp.float32)
        edge_index = jax.random.randint(ks[1], (2, N_EDGES), 0, N_NODES, dtype=jnp.int64)
        edge_types = jax.random.randint(ks[2], (N_EDGES,), 0, 2, dtype=jnp.int64)
        s = 1.0 / np.sqrt(IN_DIM)
        W_data = jax.random.uniform(ks[3], (OUT_DIM, IN_DIM), minval=-s, maxval=s, dtype=jnp.float32)
        b_data = jax.random.uniform(ks[4], (OUT_DIM,), minval=-s, maxval=s, dtype=jnp.float32)
        W_control = jax.random.uniform(ks[5], (OUT_DIM, IN_DIM), minval=-s, maxval=s, dtype=jnp.float32)
        b_control = jax.random.uniform(ks[6], (OUT_DIM,), minval=-s, maxval=s, dtype=jnp.float32)
        W_self = jax.random.uniform(ks[7], (OUT_DIM, IN_DIM), minval=-s, maxval=s, dtype=jnp.float32)
        b_self = jax.random.uniform(ks[8], (OUT_DIM,), minval=-s, maxval=s, dtype=jnp.float32)
        return {'X': X, 'edge_index': edge_index, 'edge_types': edge_types, 'W_data': W_data, 'b_data': b_data, 'W_control': W_control, 'b_control': b_control, 'W_self': W_self, 'b_self': b_self}
    _L2_gnn_all = _L2_gnn_setup()
    _L2_gnn_in = {k: v for k, v in _L2_gnn_all.items() if k in ('W_data', 'b_data', 'W_control', 'b_control', 'W_self', 'b_self')}
    del _L2_gnn_all

    def _L3_gnn_setup():
        import jax, jax.numpy as jnp
        import numpy as np
        N = 6250
        E = 100000
        D_IN = 128
        D_OUT = 128
        key = jax.random.key(seed)
        k1, k2, k3, k4 = jax.random.split(key, 4)
        x = jax.random.normal(k1, (N, D_IN), dtype=jnp.float32)
        edge_index = jax.random.randint(k2, (2, E), 0, N, dtype=jnp.int64)
        W = jax.random.normal(k3, (D_OUT, D_IN), dtype=jnp.float32) * (1.0 / np.sqrt(D_IN))
        b = jax.random.normal(k4, (D_OUT,), dtype=jnp.float32) * 0.01
        return {'x': x, 'edge_index': edge_index, 'W': W, 'b': b}
    _L3_gnn_all = _L3_gnn_setup()
    _L3_gnn_in = {k: v for k, v in _L3_gnn_all.items() if k in ('W', 'b')}
    del _L3_gnn_all
    return {'x': x, 'src': src, 'dst': dst, 'edge_type_2': edge_type_2, 'edge_type_64': edge_type_64, 'edge_weight': edge_weight, 'L0_gnn_W_self': _L0_gnn_in['W_self'], 'L0_gnn_b_self': _L0_gnn_in['b_self'], 'L0_gnn_W_msg': _L0_gnn_in['W_msg'], 'L0_gnn_b_msg': _L0_gnn_in['b_msg'], 'L0_gnn_rel_emb': _L0_gnn_in['rel_emb'], 'L1_gnn_W0': _L1_gnn_in['W0'], 'L1_gnn_b0': _L1_gnn_in['b0'], 'L1_gnn_W1': _L1_gnn_in['W1'], 'L1_gnn_b1': _L1_gnn_in['b1'], 'L1_gnn_attention': _L1_gnn_in['attention'], 'L1_gnn_scale': _L1_gnn_in['scale'], 'L1_gnn_offset': _L1_gnn_in['offset'], 'L2_gnn_W_data': _L2_gnn_in['W_data'], 'L2_gnn_b_data': _L2_gnn_in['b_data'], 'L2_gnn_W_control': _L2_gnn_in['W_control'], 'L2_gnn_b_control': _L2_gnn_in['b_control'], 'L2_gnn_W_self': _L2_gnn_in['W_self'], 'L2_gnn_b_self': _L2_gnn_in['b_self'], 'L3_gnn_W': _L3_gnn_in['W'], 'L3_gnn_b': _L3_gnn_in['b']}

def reference(x, src, dst, edge_type_2, edge_type_64, edge_weight, L0_gnn_W_self, L0_gnn_b_self, L0_gnn_W_msg, L0_gnn_b_msg, L0_gnn_rel_emb, L1_gnn_W0, L1_gnn_b0, L1_gnn_W1, L1_gnn_b1, L1_gnn_attention, L1_gnn_scale, L1_gnn_offset, L2_gnn_W_data, L2_gnn_b_data, L2_gnn_W_control, L2_gnn_b_control, L2_gnn_W_self, L2_gnn_b_self, L3_gnn_W, L3_gnn_b):
    import jax
    import jax.numpy as jnp

    def _L0_gnn_ref(node_states, edge_index, edge_type_ids, W_self, b_self, W_msg, b_msg, rel_emb):
        import jax, jax.numpy as jnp
        import numpy as np
        N_NODES = 6250
        N_EDGES = 37500
        HIDDEN = 128
        NUM_REL = 64
        src = edge_index[0]
        dst = edge_index[1]
        n_nodes = node_states.shape[0]
        rel_ids = jnp.clip(edge_type_ids, 0, rel_emb.shape[0] - 1)
        rel_vec = rel_emb[rel_ids]
        msg = (node_states[src] + rel_vec) @ W_msg.T + b_msg
        agg = jax.ops.segment_sum(msg, dst, num_segments=n_nodes)
        deg = jax.ops.segment_sum(jnp.ones((dst.shape[0],), node_states.dtype), dst, num_segments=n_nodes)
        agg = agg / jnp.maximum(deg, 1.0)[:, None]
        return node_states @ W_self.T + b_self + agg

    def _L1_gnn_ref(feat_in, edge_row, edge_col, edge_val, W0, b0, W1, b1, attention, scale, offset):
        import jax, jax.numpy as jnp
        import numpy as np
        N = 6250
        E = 100000
        DIN = 128
        DOUT = 128
        H = 4
        DS = DOUT // H

        def _lrelu(x):
            return jnp.where(x > 0, x, 0.2 * x)
        n = feat_in.shape[0]
        h_self = jax.nn.relu(feat_in @ W0.T + b0).reshape(n, H, DS)
        h_neigh = jax.nn.relu(feat_in @ W1.T + b1).reshape(n, H, DS)
        att_self = _lrelu(jnp.einsum('nhd,hd->nh', h_self, attention[0]))
        att_neigh = _lrelu(jnp.einsum('nhd,hd->nh', h_neigh, attention[1]))
        val = att_self[edge_row] + att_neigh[edge_col]
        mx = jax.ops.segment_max(val, edge_row, num_segments=n)
        val_exp = jnp.exp(val - mx[edge_row]) * edge_val[:, None]
        denom = jnp.clip(jax.ops.segment_sum(val_exp, edge_row, num_segments=n), 1e-10)
        msg = val_exp[:, :, None] * h_neigh[edge_col]
        agg = jax.ops.segment_sum(msg, edge_row, num_segments=n) / denom[:, :, None]

        def norm_feat(x, b):
            mean = x.mean(axis=-1, keepdims=True)
            var = x.var(axis=-1, keepdims=True) + 1e-09
            return (x - mean) * scale[b] * jax.lax.rsqrt(var) + offset[b]
        feat_neigh = norm_feat(agg, 0)
        feat_self = norm_feat(h_self, 1)
        return ((feat_self + feat_neigh) * 0.5).reshape(n, H * DS)

    def _L2_gnn_ref(X, edge_index, edge_types, W_data, b_data, W_control, b_control, W_self, b_self):
        import jax, jax.numpy as jnp
        import numpy as np
        IN_DIM = 128
        OUT_DIM = 128
        N_NODES = 625
        N_EDGES = 40000
        src, dst = (edge_index[0], edge_index[1])
        Xs = X[src]
        m_data = Xs @ W_data.T + b_data
        m_ctrl = Xs @ W_control.T + b_control
        msg = jnp.where((edge_types == 0)[:, None], m_data, m_ctrl)
        agg = jax.ops.segment_sum(msg, dst, num_segments=X.shape[0])
        out = agg + (X @ W_self.T + b_self)
        return jax.nn.relu(out)

    def _L3_gnn_ref(x, edge_index, W, b):
        import jax, jax.numpy as jnp
        import numpy as np
        N = 6250
        E = 100000
        D_IN = 128
        D_OUT = 128
        n = x.shape[0]
        h = jnp.einsum('nd,od->no', x, W) + b
        loop = jnp.arange(n, dtype=edge_index.dtype)
        ei = jnp.concatenate([edge_index, jnp.stack([loop, loop], axis=0)], axis=1)
        row, col = (ei[0], ei[1])
        deg = jax.ops.segment_sum(jnp.ones(row.shape, dtype=h.dtype), row, num_segments=n)
        norm = 1.0 / jnp.sqrt(deg[row] * deg[col])
        messages = norm[:, None] * h[col]
        out = jax.ops.segment_sum(messages, row, num_segments=n)
        return out
    edge_index = jnp.stack([src, dst])
    x = _layernorm(x + _L0_gnn_ref(x, edge_index, edge_type_64, L0_gnn_W_self, L0_gnn_b_self, L0_gnn_W_msg, L0_gnn_b_msg, L0_gnn_rel_emb), axis=-1)
    x = _layernorm(x + _L1_gnn_ref(x, src, dst, edge_weight, L1_gnn_W0, L1_gnn_b0, L1_gnn_W1, L1_gnn_b1, L1_gnn_attention, L1_gnn_scale, L1_gnn_offset), axis=-1)
    x = _layernorm(x + _L2_gnn_ref(x, edge_index, edge_type_2, L2_gnn_W_data, L2_gnn_b_data, L2_gnn_W_control, L2_gnn_b_control, L2_gnn_W_self, L2_gnn_b_self), axis=-1)
    x = _layernorm(x + _L3_gnn_ref(x, edge_index, L3_gnn_W, L3_gnn_b), axis=-1)
    return x

_drawn_inputs = setup_inputs


def setup_inputs(seed=0):
    import zlib

    import numpy as np

    out = dict(_drawn_inputs(seed))
    spreads = {'L1_gnn_b0': (0.0, 0.1),
     'L1_gnn_b1': (0.0, 0.1),
     'L1_gnn_scale': (1.0, 0.2),
     'L1_gnn_offset': (0.0, 0.1)}
    factors = {'L2_gnn_b_self': 3.983, 'L3_gnn_b': 6.694}
    for name, (base, spread) in spreads.items():
        noise = np.random.default_rng([zlib.crc32(name.encode()), seed]).standard_normal(out[name].shape)
        drawn = base * np.exp(spread * noise) if base else spread * noise
        out[name] = jnp.asarray(drawn.astype(out[name].dtype))
    for name, factor in factors.items():
        out[name] = (out[name] * factor).astype(out[name].dtype)
    return out
```

```python
import concourse.bass as bass
from concourse import mybir
from contextlib import ExitStack

P = 128
ALU = mybir.AluOpType
ACT = mybir.ActivationFunctionType
AX = mybir.AxisListType
F32 = mybir.dt.float32
BF16 = mybir.dt.bfloat16
I32 = mybir.dt.int32
U32 = mybir.dt.uint32
U8 = mybir.dt.uint8
RMAX = bass.bass_isa.ReduceOp.max

GROUP = 16
PAIR = 4
HEADS = 4
XW = 132
REC = 16
F_SL, F_W = 0, 1
H_DL, H_SL2, H_REL = 4, 5, 6
B_TS, B_TD = 14, 15


def gnn_four_layers_kernel(nc, t, out):
    N, D = t["x"].shape
    E = t["src"].shape[0]
    REL = t["L0_gnn_rel_emb"].shape[0]
    NT = -(-N // P)
    COLS = -(-(-(-E // P)) // (2 * GROUP)) * 2 * GROUP
    SLOTS = P * COLS
    PAD = NT * P - 1
    BUCKETS = NT * NT
    NCH = -(-((SLOTS + (P - 1) * BUCKETS) // P) // (2 * PAIR)) * 2 * PAIR
    NREC = NCH + 2 * PAIR
    assert D == P and N < NT * P and NT < P and REL <= P

    rec_d = nc.dram_tensor("records", (P * NREC, REC // 4), F32, kind="Internal").ap()
    tile_d = nc.dram_tensor("chunk_tiles", (NREC, 2), I32, kind="Internal").ap()

    with ExitStack() as ctx:
        def sb(name, shape, dt, c=ctx):
            return c.enter_context(nc.sbuf_tensor(name, shape, dt))

        def sem(name, c=ctx):
            return c.enter_context(nc.semaphore(name))

        def ps(name, shape, c, dt=F32):
            return c.enter_context(nc.psum_tensor(name, shape, dt))

        passed = sem("passed")

        def apart(eng):
            eng.sem_inc(passed, 1)

        iota_f = sb("iota_f", [P, P], F32)
        iota_b = sb("iota_b", [P, 2 * P], BF16)
        ident_f = sb("ident_f", [P, P], F32)
        ident_b = sb("ident_b", [P, P], BF16)
        zero_b = sb("zero_b", [P, P], BF16)
        eps = sb("eps", [P, 2], F32)
        deg_out = sb("deg_out", [P, NT], F32)
        deg_in = sb("deg_in", [P, NT], F32)

        with ExitStack() as c1:
            ones_f = sb("ones_f", [P, P], F32, c1)
            before = sb("before", [P, P], F32, c1)
            after = sb("after", [P, P], F32, c1)
            esrc = sb("esrc", [P, COLS], I32, c1)
            edst = sb("edst", [P, COLS], I32, c1)
            ety2 = sb("ety2", [P, COLS], I32, c1)
            ety64 = sb("ety64", [P, COLS], I32, c1)
            ew = sb("ew", [P, COLS], F32, c1)
            tmp = sb("tmp", [P, COLS], I32, c1)
            ts_b = sb("ts_b", [P, COLS + GROUP], BF16, c1)
            td_b = sb("td_b", [P, COLS + GROUP], BF16, c1)
            sl_b = sb("sl_b", [P, COLS], BF16, c1)
            key = sb("key", [P, COLS + GROUP], F32, c1)
            rec = sb("rec", [P, COLS, REC // 4], F32, c1)
            null = sb("null", [P, 8 * GROUP, REC // 4], F32, c1)
            first = sb("first", [NT, NT], F32, c1)
            rec_h = rec[:, :, :].bitcast(BF16)
            rec_8 = rec[:, :, :].bitcast(U8)
            null_h = null[:, :, :].bitcast(BF16)
            null_8 = null[:, :, :].bitcast(U8)

            loads = sem("loads", c1)
            pads = sem("pads", c1)
            consts = sem("consts", c1)
            pool_step = sem("pool_step", c1)
            prep = sem("prep", c1)
            null_ok = sem("null_ok", c1)
            nulled = sem("nulled", c1)

            with nc.Block() as block:
                full = E // COLS
                rest = E - full * COLS

                @block.sync
                def _(sp):
                    sp.wait_ge(pads, 5)
                    for tl, name in ((esrc, "src"), (edst, "dst"), (ety2, "edge_type_2"),
                                     (ety64, "edge_type_64"), (ew, "edge_weight")):
                        sp.dma_start(tl[0:full, :], t[name][0:full * COLS].rearrange("(p c) -> p c", c=COLS)).then_inc(loads, 16)
                        if rest:
                            sp.dma_start(tl[full:full + 1, 0:rest], t[name][full * COLS:E].rearrange("(p c) -> p c", p=1)).then_inc(loads, 16)
                    sp.wait_ge(null_ok, 4)
                    r = rec_d.rearrange("(p c) w -> p (c w)", p=P)
                    W = REC // 4
                    step = 8 * GROUP
                    n = 0
                    for a in range(0, NREC, step):
                        b = min(a + step, NREC)
                        sp.dma_start(r[:, a * W:b * W], null[:, 0:b - a, :].rearrange("p c w -> p (c w)")).then_inc(nulled, 16)
                        n += 16
                    sp.wait_ge(nulled, n)

                @block.gpsimd
                def _(gp):
                    gp.iota(iota_f[:, :], pattern=[[1, P]], base=0, channel_multiplier=0,
                            allow_small_or_imprecise_dtypes=True).then_inc(consts, 1)
                    gp.iota(iota_b[:, :], pattern=[[1, 2 * P]], base=0, channel_multiplier=0,
                            allow_small_or_imprecise_dtypes=True).then_inc(consts, 1)
                    for m, v in ((ident_f, 0.0), (ident_b, 0.0), (before, 1.0), (after, 1.0)):
                        gp.memset(m[:, :], v).then_inc(pool_step, 1)
                    gp.memset(ones_f[:, :], 1.0).then_inc(consts, 1)
                    gp.memset(zero_b[:, :], 0.0).then_inc(consts, 1)
                    gp.memset(eps[:, 0:1], 1e-5).then_inc(consts, 1)
                    gp.memset(eps[:, 1:2], 1e-9).then_inc(consts, 1)
                    gp.wait_ge(pool_step, 4)
                    for m in (ident_f, ident_b):
                        gp.affine_select(out=m[:, :], in_=m[:, :], compare_op=ALU.not_equal, fill=1.0,
                                         base=0, pattern=[[-1, P]], channel_multiplier=1).then_inc(consts, 1)
                    gp.affine_select(out=before[:, :], in_=before[:, :], compare_op=ALU.is_gt, fill=0.0,
                                     base=0, pattern=[[-1, P]], channel_multiplier=1).then_inc(consts, 1)
                    gp.affine_select(out=after[:, :], in_=after[:, :], compare_op=ALU.is_gt, fill=0.0,
                                     base=0, pattern=[[1, P]], channel_multiplier=-1).then_inc(consts, 1)

                @block.vector
                def _(v):
                    n = [0]

                    def link(ins):
                        n[0] += 1
                        ins.then_inc(prep, 1)
                        v.wait_ge(prep, n[0])

                    v.memset(esrc[:, :], PAD).then_inc(pads, 1)
                    v.memset(edst[:, :], PAD).then_inc(pads, 1)
                    v.memset(ety2[:, :], 0).then_inc(pads, 1)
                    v.memset(ety64[:, :], 0).then_inc(pads, 1)
                    v.memset(ew[:, :], 0.0).then_inc(pads, 1)
                    link(v.memset(null[:, :, :], 0.0))
                    v.memset(null[:, :, F_SL:F_SL + 1], -1.0).then_inc(null_ok, 1)
                    v.memset(null_h[:, :, H_DL:H_DL + 1], -1.0).then_inc(null_ok, 1)
                    v.memset(null_h[:, :, H_SL2:H_SL2 + 1], -1.0).then_inc(null_ok, 1)
                    v.memset(null_h[:, :, H_REL:H_REL + 1], -1.0).then_inc(null_ok, 1)
                    v.wait_ge(loads, 16 * 5 * (2 if rest else 1))
                    link(v.tensor_scalar(tmp[:, :], esrc[:, :], 7, None, ALU.logical_shift_right))
                    for a in (ts_b, td_b, key):
                        link(v.memset(a[:, COLS:COLS + GROUP], 0.0))
                    link(v.tensor_copy(ts_b[:, 0:COLS], tmp[:, :]))
                    link(v.tensor_copy(rec_8[:, :, B_TS], tmp[:, :]))
                    link(v.tensor_scalar(key[:, 0:COLS], tmp[:, :], float(NT), None, ALU.mult))
                    link(v.tensor_scalar(tmp[:, :], edst[:, :], 7, None, ALU.logical_shift_right))
                    link(v.tensor_copy(td_b[:, 0:COLS], tmp[:, :]))
                    link(v.tensor_copy(rec_8[:, :, B_TD], tmp[:, :]))
                    link(v.tensor_tensor(key[:, 0:COLS], key[:, 0:COLS], tmp[:, :], ALU.add))
                    link(v.tensor_scalar(tmp[:, :], edst[:, :], P - 1, None, ALU.bitwise_and))
                    link(v.tensor_copy(rec_h[:, :, H_DL], tmp[:, :]))
                    link(v.tensor_scalar(tmp[:, :], esrc[:, :], P - 1, None, ALU.bitwise_and))
                    link(v.tensor_copy(rec[:, :, F_SL], tmp[:, :]))
                    link(v.tensor_copy(sl_b[:, :], tmp[:, :]))
                    link(v.tensor_copy(rec[:, :, F_W], ew[:, :]))
                    link(v.tensor_scalar(ety2[:, :], ety2[:, :], 0.0, float(P), ALU.not_equal, ALU.mult))
                    link(v.tensor_tensor(rec_h[:, :, H_SL2], ety2[:, :], tmp[:, :], ALU.add))
                    link(v.tensor_scalar(rec_h[:, :, H_REL], ety64[:, :], 0.0, float(REL - 1), ALU.max, ALU.min))
                    v.wait_ge(consts, 10)

            with ExitStack() as c2:
                pH = ps("pH", [NT, 512], c2)
                pOut = ps("pOut", [NT, 512], c2)
                pIn = ps("pIn", [NT, 512], c2)
                pB = ps("pB", [P, 512], c2)
                pD = ps("pD", [P, 512], c2)
                hts = sb("hts", [P, 2, GROUP, NT], BF16, c2)
                htd = sb("htd", [P, 2, GROUP, NT], BF16, c2)
                hsl = sb("hsl", [P, 2, GROUP, P], BF16, c2)
                hdl = sb("hdl", [P, 2, GROUP, P], BF16, c2)
                cnt = sb("cnt", [NT, NT], F32, c2)
                cnti = sb("cnti", [NT, NT], I32, c2)
                incl = sb("incl", [NT, NT], F32, c2)
                dego = sb("dego", [NT, P], F32, c2)
                degi = sb("degi", [NT, P], F32, c2)
                degs = sb("degs", [P, 2, NT], F32, c2)
                hot = sem("hot", c2)
                counted = sem("counted", c2)
                ostep = sem("ostep", c2)
                tri_done = sem("tri_done", c2)
                deg_t = sem("deg_t", c2)
                sq = sem("sq", c2)
                HN = COLS // (2 * GROUP)
                with nc.Block() as block:
                    @block.vector
                    def _(v):
                        def onehots(g_first, par):
                            cols = bass.ds(g_first, GROUP)
                            for o, src, w in ((hts, ts_b, NT), (htd, td_b, NT), (hsl, sl_b, P), (hdl, None, P)):
                                s = (rec_h[:, cols, H_DL] if src is None else src[:, cols])
                                ins = v.tensor_tensor(o[:, par, :, :], iota_b[:, 0:w].unsqueeze(1).broadcast_to([P, GROUP, w]),
                                                      s.unsqueeze(2).broadcast_to([P, GROUP, w]), ALU.is_equal)
                            ins.then_inc(hot, 1)

                        with v.Fori(0, HN) as i:
                            for par in range(2):
                                v.wait_ge(counted, 2 * i + par + 1)
                                onehots(i * 2 * GROUP + par * GROUP, par)
                        v.wait_ge(counted, 2 * HN + 3)
                        n = [0]

                        def link(ins):
                            n[0] += 1
                            ins.then_inc(ostep, 1)
                            v.wait_ge(ostep, n[0])

                        link(v.tensor_scalar(cnti[:, :], pH[:, 0:NT], float(P - 1), None, ALU.add))
                        link(v.tensor_scalar(cnti[:, :], cnti[:, :], 7, None, ALU.logical_shift_right))
                        link(v.tensor_copy(cnt[:, :], cnti[:, :]))
                        link(v.tensor_tensor_scan(incl[:, :], ones_f[0:NT, 0:NT], cnt[:, :], 0.0, ALU.mult, ALU.add))
                        link(v.tensor_tensor(cnt[:, :], incl[:, :], cnt[:, :], ALU.subtract))
                        link(v.tensor_copy(dego[:, :], pOut[:, 0:P]))
                        link(v.tensor_copy(degi[:, :], pIn[:, 0:P]))
                        v.wait_ge(tri_done, 1)
                        link(v.tensor_scalar(first[:, :], cnt[:, :], pB[0:NT, 0:1], float(P), ALU.add, ALU.mult))
                        v.wait_ge(deg_t, 2)
                        link(v.tensor_scalar(degs[:, 0, :], pD[:, 128:128 + NT], 1.0, None, ALU.add))
                        link(v.tensor_scalar(degs[:, 1, :], pD[:, 256:256 + NT], 1.0, None, ALU.max))
                        link(v.reciprocal(deg_in[:, :], degs[:, 1, :]))
                        v.wait_ge(sq, 1)
                        link(v.reciprocal(deg_out[:, :], degs[:, 0, :]))

                    @block.tensor
                    def _(pe):
                        pe.matmul(pH[:, 0:NT], zero_b[:, 0:NT], zero_b[:, 0:NT], start=True, stop=False, skip_group_check=True)
                        pe.matmul(pOut[:, 0:P], zero_b[:, 0:NT], zero_b[:, 0:P], start=True, stop=False, skip_group_check=True)
                        pe.matmul(pIn[:, 0:P], zero_b[:, 0:NT], zero_b[:, 0:P], start=True, stop=False, skip_group_check=True).then_inc(counted, 2)
                        with pe.Fori(0, HN) as i:
                            for par in range(2):
                                pe.wait_ge(hot, 2 * i + par + 1)
                                for k in range(GROUP):
                                    pe.matmul(pH[:, 0:NT], hts[:, par, k, :], htd[:, par, k, :], start=False, stop=False, skip_group_check=True)
                                    pe.matmul(pOut[:, 0:P], hts[:, par, k, :], hsl[:, par, k, :], start=False, stop=False, skip_group_check=True)
                                    mm = pe.matmul(pIn[:, 0:P], htd[:, par, k, :], hdl[:, par, k, :], start=False, stop=False, skip_group_check=True)
                                mm.then_inc(counted, 1)
                        pe.matmul(pH[:, 0:NT], zero_b[:, 0:NT], zero_b[:, 0:NT], start=False, stop=True, skip_group_check=True)
                        pe.matmul(pOut[:, 0:P], zero_b[:, 0:NT], zero_b[:, 0:P], start=False, stop=True, skip_group_check=True)
                        pe.matmul(pIn[:, 0:P], zero_b[:, 0:NT], zero_b[:, 0:P], start=False, stop=True, skip_group_check=True).then_inc(counted, 1)
                        pe.wait_ge(ostep, 7)
                        pe.matmul(pB[0:NT, 0:1], after[0:NT, 0:NT], incl[:, NT - 1:NT], start=True, stop=True).then_inc(tri_done, 1)
                        pe.transpose(pD[:, 128:128 + NT], dego[:, :], ident_f[0:NT, 0:NT]).then_inc(deg_t, 1)
                        pe.transpose(pD[:, 256:256 + NT], degi[:, :], ident_f[0:NT, 0:NT]).then_inc(deg_t, 1)

                    @block.scalar
                    def _(act):
                        act.wait_ge(ostep, 9)
                        act.activation(degs[:, 0, :], degs[:, 0, :], ACT.Sqrt).then_inc(sq, 1)

            with ExitStack() as c2:
                hts = sb("hts2", [P, 2, GROUP, NT], BF16, c2)
                htd = sb("htd2", [P, 2, GROUP, NT], BF16, c2)
                diag = sb("diag", [P, 2, P], F32, c2)
                hT = sb("hT", [NT, 2, P], F32, c2)
                run = sb("run", [NT, 2, NT], F32, c2)
                junk = sb("junk", [P, 2, P], F32, c2)
                junk2 = sb("junk2", [P, 2, NT], F32, c2)
                rank = sb("rank", [P, 2, GROUP], F32, c2)
                base = sb("base", [P, 2, GROUP], F32, c2)
                pos = sb("pos", [P, GROUP], I32, c2)
                posl = sb("posl", [P, GROUP], I32, c2)
                posh = sb("posh", [P, GROUP], I32, c2)
                idx = sb("idx", [P, 2, GROUP], U32, c2)
                ring = sb("ring", [P, 2, GROUP, REC // 4], F32, c2)
                pK = [ps(f"pK{i}", [P, 512], c2) for i in range(2)]
                pT = [ps(f"pT{i}", [P, 512], c2) for i in range(2)]
                pG = [ps(f"pG{i}", [P, 512], c2) for i in range(2)]
                pR = ps("pR", [P, 512], c2)

                DEPTH = 2
                s_hot = sem("s_hot", c2)
                s_hot_free = sem("s_hot_free", c2)
                s_diag = sem("s_diag", c2)
                s_krow = sem("s_krow", c2)
                s_tr = sem("s_tr", c2)
                s_ht = sem("s_ht", c2)
                s_run = sem("s_run", c2)
                s_look = sem("s_look", c2)
                s_add = sem("s_add", c2)
                s_rank = sem("s_rank", c2)
                s_base = sem("s_base", c2)
                s_pos = sem("s_pos", c2)
                s_idx = sem("s_idx", c2)
                s_ring = sem("s_ring", c2)
                s_sent = [sem(f"s_sent{i}", c2) for i in range(2)]
                NG2 = COLS // (2 * GROUP)

                with nc.Block() as block:
                    @block.vector
                    def _(v):
                        v.sem_inc(s_rank, DEPTH)
                        v.sem_inc(s_base, DEPTH)

                        def hot(g, par):
                            v.wait_ge(s_hot_free, g + 1)
                            for o, src in ((hts, ts_b), (htd, td_b)):
                                ins = v.tensor_tensor(o[:, par, :, :], iota_b[:, 0:NT].unsqueeze(1).broadcast_to([P, GROUP, NT]),
                                                      src[:, bass.ds(g * GROUP, GROUP)].unsqueeze(2).broadcast_to([P, GROUP, NT]), ALU.is_equal)
                            ins.then_inc(s_hot, 1)

                        def diagonal(c, b):
                            v.tensor_scalar(diag[:, b, :], ident_f[:, :], key[:, bass.ds(c, 1)], None, ALU.mult).then_inc(s_diag, 1)

                        hot(0, 0)
                        diagonal(0, 0)
                        diagonal(1, 1)
                        with v.Fori(0, NG2) as i:
                            for par in range(2):
                                g = 2 * i + par
                                for k in range(GROUP):
                                    c = g * GROUP + k
                                    v.wait_ge(s_krow, c + 3)
                                    v.scalar_tensor_tensor(out=junk[:, k % 2, :], in0=pK[k % 2][:, 0:P], scalar=key[:, bass.ds(c, 1)], in1=before[:, :],
                                                           op0=ALU.is_equal, op1=ALU.mult, accum_out=rank[:, par, k:k + 1]).then_inc(s_rank, 1)
                                    diagonal(c + 2, k % 2)
                                    v.wait_ge(s_look, c + 3)
                                    v.scalar_tensor_tensor(out=junk2[:, k % 2, :], in0=pG[k % 2][:, 0:NT], scalar=1.0, in1=htd[:, par, k, :],
                                                           op0=ALU.mult, op1=ALU.mult, accum_out=base[:, par, k:k + 1]).then_inc(s_base, 1)
                                    if k == 4:
                                        hot(g + 1, 1 - par)
                                v.wait_ge(s_rank, g * GROUP + GROUP + 2)
                                v.wait_ge(s_base, g * GROUP + GROUP + 2)
                                v.tensor_tensor(pos[:, :], rank[:, par, :], base[:, par, :], ALU.add).then_inc(s_pos, 1)
                                v.wait_ge(s_pos, g * 4 + 1)
                                v.tensor_scalar(posl[:, :], pos[:, :], P - 1, None, ALU.bitwise_and).then_inc(s_pos, 1)
                                v.tensor_scalar(posh[:, :], pos[:, :], 7, None, ALU.logical_shift_right).then_inc(s_pos, 1)
                                v.wait_ge(s_pos, g * 4 + 3)
                                v.wait_ge(s_sent[par], i * (16 * GROUP) + 16)
                                v.scalar_tensor_tensor(out=idx[:, par, :], in0=posl[:, :], scalar=float(NREC), in1=posh[:, :],
                                                       op0=ALU.mult, op1=ALU.add).then_inc(s_idx, 1)
                                v.sem_inc(s_pos, 1)

                    @block.tensor
                    def _(pe):
                        pe.sem_inc(s_hot_free, DEPTH)
                        pe.sem_inc(s_krow, DEPTH)
                        pe.sem_inc(s_tr, DEPTH)
                        pe.sem_inc(s_look, DEPTH)
                        pe.matmul(pR[0:NT, 0:NT], zero_b[:, 0:NT], zero_b[:, 0:NT], start=True, stop=False, skip_group_check=True).then_inc(s_add, 1)

                        def keys_and_turn(c, k, par):
                            pe.wait_ge(s_diag, c + 1)
                            pe.wait_ge(s_rank, c + 1)
                            pe.matmul(pK[k % 2][:, 0:P], ones_f[:, :], diag[:, k % 2, :], start=True, stop=True).then_inc(s_krow, 1)
                            pe.wait_ge(s_ht, c + 1)
                            pe.matmul(pT[k % 2][0:NT, 0:P], hts[:, par, k, :], ident_b[:, :], start=True, stop=True).then_inc(s_tr, 1)

                        pe.wait_ge(s_hot, 1)
                        keys_and_turn(0, 0, 0)
                        with pe.Fori(0, NG2) as i:
                            for par in range(2):
                                g = 2 * i + par
                                for k in range(GROUP):
                                    c = g * GROUP + k
                                    if k + 1 < GROUP:
                                        keys_and_turn(c + 1, k + 1, par)
                                    else:
                                        pe.wait_ge(s_hot, g + 2)
                                        keys_and_turn(c + 1, 0, 1 - par)
                                    pe.wait_ge(s_ht, c + 3)
                                    pe.wait_ge(s_run, c + 1)
                                    pe.wait_ge(s_base, c + 1)
                                    pe.matmul(pG[k % 2][:, 0:NT], hT[:, k % 2, :], first[:, :], start=True, stop=False)
                                    pe.matmul(pG[k % 2][:, 0:NT], hT[:, k % 2, :], run[:, k % 2, :], start=False, stop=True).then_inc(s_look, 1)
                                    mm = pe.matmul(pR[0:NT, 0:NT], hts[:, par, k, :], htd[:, par, k, :], start=False, stop=False, skip_group_check=True)
                                    mm.then_inc(s_add, 1)
                                pe.wait_ge(s_add, g * GROUP + GROUP + 1)
                                pe.sem_inc(s_hot_free, 1)
                        pe.matmul(pR[0:NT, 0:NT], zero_b[:, 0:NT], zero_b[:, 0:NT], start=False, stop=True, skip_group_check=True)

                    @block.scalar
                    def _(act):
                        act.sem_inc(s_ht, DEPTH)

                        def turned(c, k):
                            act.wait_ge(s_tr, c + 3)
                            act.wait_ge(s_look, c + 1)
                            act.activation(hT[:, k % 2, :], pT[k % 2][0:NT, 0:P], ACT.Copy).then_inc(s_ht, 1)

                        turned(0, 0)
                        with act.Fori(0, NG2) as i:
                            for par in range(2):
                                g = 2 * i + par
                                for k in range(GROUP):
                                    c = g * GROUP + k
                                    act.wait_ge(s_add, c + 1)
                                    act.wait_ge(s_look, c + 1)
                                    act.activation(run[:, k % 2, :], pR[0:NT, 0:NT], ACT.Copy).then_inc(s_run, 1)
                                    turned(c + 1, k + 1)
                                act.wait_ge(s_sent[par], i * (16 * GROUP) + 16)
                                apart(act)
                                act.copy(ring[:, par, :, :].rearrange("p c w -> p (c w)").bitcast(I32),
                                         rec[:, bass.ds(g * GROUP, GROUP), :].rearrange("p c w -> p (c w)").bitcast(I32)).then_inc(s_ring, 1)

                    @block.gpsimd
                    def _(gp):
                        for par in range(2):
                            gp.dma_start(rec_d[NREC - 1 - par:NREC - par, :], null[0:1, 0, :]).then_inc(s_sent[par], 16)
                        with gp.Fori(0, NG2) as i:
                            for par in range(2):
                                g = 2 * i + par
                                gp.wait_ge(s_idx, g + 1)
                                gp.wait_ge(s_ring, g + 1)
                                apart(gp)
                                for k in range(GROUP):
                                    gp.indirect_dma_start(rec_d, bass.IndirectOffsetOnAxis(ap=idx[:, par, k:k + 1], axis=0),
                                                          ring[:, par, k, :], None).then_inc(s_sent[par], 16)
                        gp.wait_ge(s_sent[0], NG2 * 16 * GROUP + 16)
                        gp.wait_ge(s_sent[1], NG2 * 16 * GROUP + 16)

        recs = sb("recs", [P, NREC, REC // 4], F32)
        recs_h = recs[:, :, :].bitcast(BF16)
        recs_8 = recs[:, :, :].bitcast(U8)
        relx = sb("relx", [REL, 3, P], BF16)
        B = sb("B", [P, NT, P], F32)
        acc = sb("acc", [P, NT, XW], F32)
        X = sb("X", [P, NT, 3, P], BF16)
        with ExitStack() as c1:
            tiles = sb("tiles", [1, NREC, 2], I32, c1)
            s_recs = sem("s_recs", c1)
            s_tiles = sem("s_tiles", c1)
            s_tsent = sem("s_tsent", c1)
            with nc.Block() as block:
                @block.sync
                def _(sp):
                    sp.dma_start(recs[:, :, :].rearrange("p c w -> p (c w)"), rec_d.rearrange("(p c) w -> p (c w)", p=P)).then_inc(s_recs, 16)
                    sp.wait_ge(s_tiles, 1)
                    sp.dma_start(tile_d.rearrange("(a c) b -> a (c b)", a=1), tiles[:, :, :].rearrange("p c b -> p (c b)")).then_inc(s_tsent, 16)
                    sp.wait_ge(s_tsent, 16)

                @block.vector
                def _(v):
                    v.wait_ge(s_recs, 16)
                    v.tensor_copy(tiles[:, :, :], recs_8[0:1, :, B_TS:B_TD + 1]).then_inc(s_tiles, 1)

        def aggregate(mode, name):
            by_source = mode in ("relation", "typed")
            wide = 2 * P if by_source else P
            cdt = F32 if mode == "weighted" else BF16
            width = XW if mode == "weighted" else P
            NG = NCH // PAIR
            with ExitStack() as c:
                h1 = sb(f"h1{name}", [P, 2, PAIR, 2 * P if mode == "typed" else P], cdt, c)
                h2 = sb(f"h2{name}", [P, 2, PAIR, P], cdt, c)
                h3 = sb(f"h3{name}", [P, 2, PAIR, 64], BF16, c) if mode == "relation" else None
                dl = sb(f"dl{name}", [P, 2, PAIR], BF16, c)
                Cs = sb(f"Cs{name}", [P, 2, PAIR, wide], cdt, c)
                pC = [ps(f"pC{name}{i}", [P, PAIR, wide], c) for i in range(2)]
                pO = [ps(f"pO{name}{i}", [P, PAIR, 2 * P], c) for i in range(2)]
                iota = iota_f if mode == "weighted" else iota_b
                s_h1 = sem(f"s_h1{name}", c)
                s_h2 = sem(f"s_h2{name}", c)
                s_dl = sem(f"s_dl{name}", c)
                s_c = sem(f"s_c{name}", c)
                s_cs = sem(f"s_cs{name}", c)
                s_o = sem(f"s_o{name}", c)
                s_acc = sem(f"s_acc{name}", c)

                with nc.Block() as block:
                    @block.vector
                    def _(v):
                        v.sem_inc(s_acc, 2 * PAIR)

                        def hot(g, par):
                            v.wait_ge(s_c, g + 1)
                            for k in range(PAIR):
                                ch = g * PAIR + k
                                f32 = recs[:, bass.ds(ch, 1), F_SL:F_W + 1].rearrange("p a w -> p (a w)")
                                h16 = recs_h[:, bass.ds(ch, 1), H_DL:H_REL + 1].rearrange("p a w -> p (a w)")
                                if mode == "weighted":
                                    ins = v.tensor_scalar(h1[:, par, k, :], iota[:, 0:P], f32[:, 0:1], f32[:, 1:2], ALU.is_equal, ALU.mult)
                                elif mode == "typed":
                                    ins = v.tensor_scalar(h1[:, par, k, :], iota[:, :], h16[:, 1:2], None, ALU.is_equal)
                                else:
                                    ins = v.tensor_scalar(h1[:, par, k, :], iota[:, 0:P], f32[:, 0:1], None, ALU.is_equal)
                                if mode == "relation":
                                    ins = v.tensor_scalar(h3[:, par, k, :], iota[:, 0:64], h16[:, 2:3], None, ALU.is_equal)
                            ins.then_inc(s_h1, 1)

                        hot(0, 0)
                        hot(1, 1)
                        with v.Fori(0, NG // 2) as i:
                            for par in range(2):
                                g = 2 * i + par
                                hot(g + 2, par)
                                bs = [v.value_load(tile_d[bass.ds(g * PAIR + k, 1), (1 if by_source else 0):(2 if by_source else 1)], min_val=0, max_val=NT - 1) for k in range(PAIR)]
                                v.wait_ge(s_o, g + 3)
                                for k in range(PAIR):
                                    v.wait_ge(s_acc, (g + 2) * PAIR + k)
                                    dst = acc[:, bass.ds(bs[k], 1), 0:width].rearrange("p a w -> p (a w)")
                                    v.tensor_tensor(dst, dst, pO[par][:, k, 0:width], ALU.add).then_inc(s_acc, 1)

                    @block.gpsimd
                    def _(gp):
                        def hot(g, par):
                            gp.wait_ge(s_c, g + 1)
                            gp.tensor_copy(dl[:, par, :], recs_h[:, bass.ds(g * PAIR, PAIR), H_DL]).then_inc(s_dl, 1)
                            gp.wait_ge(s_dl, g + 1)
                            apart(gp)
                            for k in range(PAIR):
                                ins = gp.tensor_scalar(h2[:, par, k, :], iota[:, 0:P], dl[:, par, k:k + 1], None, ALU.is_equal)
                            ins.then_inc(s_h2, 1)

                        hot(0, 0)
                        hot(1, 1)
                        with gp.Fori(0, NG // 2) as i:
                            for par in range(2):
                                hot(2 * i + par + 2, par)

                    @block.scalar
                    def _(act):
                        act.sem_inc(s_cs, DEPTH)

                        def evacuate(g, par):
                            act.wait_ge(s_c, g + 3)
                            act.wait_ge(s_o, g + 1)
                            if mode == "relation":
                                act.activation(Cs[:, par, :, 0:P], pC[par][:, :, 0:P], ACT.Copy)
                                act.activation(Cs[0:64, par, :, P:2 * P], pC[par][0:64, :, P:2 * P], ACT.Copy).then_inc(s_cs, 1)
                            else:
                                act.activation(Cs[:, par, :, :], pC[par][:, :, :], ACT.Copy).then_inc(s_cs, 1)

                        evacuate(0, 0)
                        with act.Fori(0, NG // 2) as i:
                            for par in range(2):
                                evacuate(2 * i + par + 1, 1 - par)

                    @block.tensor
                    def _(pe):
                        pe.sem_inc(s_c, DEPTH)
                        pe.sem_inc(s_o, DEPTH)

                        def table(g, par):
                            pe.wait_ge(s_h1, g + 1)
                            pe.wait_ge(s_h2, g + 1)
                            pe.wait_ge(s_cs, g + 1)
                            for k in range(PAIR):
                                if by_source:
                                    mm = pe.matmul(pC[par][:, k, 0:P], h1[:, par, k, 0:P], h2[:, par, k, :], start=True, stop=True)
                                    if mode == "relation":
                                        mm = pe.matmul(pC[par][0:64, k, P:2 * P], h3[:, par, k, :], h2[:, par, k, :], start=True, stop=True)
                                    else:
                                        mm = pe.matmul(pC[par][:, k, P:2 * P], h1[:, par, k, P:2 * P], h2[:, par, k, :], start=True, stop=True)
                                else:
                                    mm = pe.matmul(pC[par][:, k, :], h2[:, par, k, :], h1[:, par, k, :], start=True, stop=True)
                            mm.then_inc(s_c, 1)

                        table(0, 0)
                        with pe.Fori(0, NG // 2) as i:
                            for par in range(2):
                                g = 2 * i + par
                                table(g + 1, 1 - par)
                                As = [pe.value_load(tile_d[bass.ds(g * PAIR + k, 1), (0 if by_source else 1):(1 if by_source else 2)], min_val=0, max_val=NT - 1) for k in range(PAIR)]
                                pe.wait_ge(s_cs, g + 3)
                                pe.wait_ge(s_acc, g * PAIR + PAIR)
                                for k in range(PAIR):
                                    o = pO[par][:, k, 0:width]
                                    if mode == "weighted":
                                        mm = pe.matmul(o, Cs[:, par, k, :], Xw[:, bass.ds(As[k], 1), :].rearrange("p a w -> p (a w)"), start=True, stop=True)
                                    else:
                                        for s in range(3):
                                            mm = pe.matmul(o, Cs[:, par, k, 0:P], X[:, bass.ds(As[k], 1), s, :].rearrange("p a w -> p (a w)"),
                                                           start=(s == 0), stop=(s == 2 and not by_source))
                                        if mode == "relation":
                                            for s in range(3):
                                                mm = pe.matmul(o, Cs[0:64, par, k, P:2 * P], relx[:, s, :], start=False, stop=(s == 2))
                                        if mode == "typed":
                                            for s in range(3):
                                                mm = pe.matmul(o, Cs[:, par, k, P:2 * P], X2[:, bass.ds(As[k], 1), s, :].rearrange("p a w -> p (a w)"),
                                                               start=False, stop=(s == 2))
                                mm.then_inc(s_o, 1)

        Xw = X[:, :, :, :].rearrange("p t s d -> p (t s d)").bitcast(F32)[:, 0:NT * XW].rearrange("p (t w) -> p t w", w=XW)
        G7 = max(d for d in range(1, 9) if NT % d == 0)
        WEIGHTS = [["L0_gnn_W_msg", "L0_gnn_W_self"], ["L1_gnn_W1", "L1_gnn_W0"],
                   ["L2_gnn_W_data", "L2_gnn_W_control", "L2_gnn_W_self"], ["L3_gnn_W"], []]
        VECTORS = [["L0_gnn_b_msg", "L0_gnn_b_self"], ["L1_gnn_b1", "L1_gnn_b0", "att", "scale1", "off1"],
                   ["L2_gnn_b_data", "L2_gnn_b_control", "L2_gnn_b_self", "scale0", "off0"], ["L3_gnn_b"], []]
        DV = P // HEADS

        def vector_of(name):
            if name == "att":
                return t["L1_gnn_attention"][1, :, :].rearrange("h d -> (h d)")
            if name[:-1] in ("scale", "off"):
                return t["L1_gnn_scale" if name[0] == "s" else "L1_gnn_offset"][int(name[-1]), :, :].rearrange("h d -> (h d)")
            return t[name]

        def node_stage(k):
            nW, nV = len(WEIGHTS[k]), len(VECTORS[k])
            with ExitStack() as c:
                WT = sb(f"WT{k}", [P, max(nW, 1), P], F32, c)
                vec = sb(f"vec{k}", [P, max(nV, 1), P], F32, c)
                W1 = sb(f"W1_{k}", [P, G7, P], F32, c)
                xT = sb(f"xT{k}", [P, G7, P], F32, c)
                st = sb(f"st{k}", [P, G7, 6], F32, c)
                mv = sb(f"mv{k}", [P, G7, 2], F32, c)
                sd = sb(f"sd{k}", [P, G7], F32, c)
                m4 = sb(f"m4_{k}", [P, G7, HEADS], F32, c)
                v4 = sb(f"v4_{k}", [P, G7, HEADS], F32, c)
                gm = sb(f"gm{k}", [P, 2, HEADS], F32, c)
                pT = ps(f"pT_{k}", [P, 8, P], c)
                pY = [ps(f"pY_{k}{j}", [P, 8, P], c) for j in range(3)]
                s_load = sem(f"s_load{k}", c)
                s_wt = sem(f"s_wt{k}", c)
                s_wc = sem(f"s_wc{k}", c)
                s_rel = sem(f"s_rel{k}", c)
                s_relv = sem(f"s_relv{k}", c)
                s_link = sem(f"s_link{k}", c)
                s_ask = sem(f"s_ask{k}", c)
                s_sqrt = sem(f"s_sqrt{k}", c)
                s_new = sem(f"s_new{k}", c)
                s_tp = sem(f"s_tp{k}", c)
                s_xt = sem(f"s_xt{k}", c)
                s_y = sem(f"s_y{k}", c)
                s_done = sem(f"s_done{k}", c)
                s_out = sem(f"s_out{k}", c)
                scale_n = 1 if k < 4 else 0

                with nc.Block() as block:
                    @block.sync
                    def _(sp):
                        n = 0
                        for j, w in enumerate(WEIGHTS[k]):
                            sp.dma_start(W1[:, j, :], t[w]).then_inc(s_load, 16)
                            n += 16
                        for j, b in enumerate(VECTORS[k]):
                            sp.dma_start(vec[:, j, :], vector_of(b).rearrange("(a n) -> a n", a=1).broadcast_to([P, P])).then_inc(s_load, 16)
                            n += 16
                        if k == 0:
                            sp.dma_start(W1[0:REL, 3, :], t["L0_gnn_rel_emb"]).then_inc(s_load, 16)
                            full = N // P
                            sp.dma_start(B[:, 0:full, :], t["x"][0:full * P, :].rearrange("(t p) d -> p t d", p=P)).then_inc(s_load, 16)
                            sp.wait_ge(s_link, 1)
                            sp.dma_start(B[0:N - full * P, full, :], t["x"][full * P:N, :]).then_inc(s_load, 16)
                            n += 48
                        if n:
                            sp.wait_ge(s_load, n)

                    @block.tensor
                    def _(pe):
                        if nW:
                            pe.wait_ge(s_load, 16 * (nW + nV) + (48 if k == 0 else 0))
                            for j in range(nW):
                                pe.transpose(pT[:, j, :], W1[:, j, :], ident_f[:, :]).then_inc(s_wt, 1)
                        if k == 0:
                            pe.transpose(pT[:, 3, 0:REL], W1[0:REL, 3, :], ident_f[0:REL, 0:REL]).then_inc(s_wt, 1)
                            pe.wait_ge(s_wc, 2)
                            pe.matmul(pT[0:REL, 4, :], xT[:, 0, 0:REL], WT[:, 0, :], start=True, stop=True).then_inc(s_rel, 1)

                    @block.scalar
                    def _(act):
                        if nW:
                            act.wait_ge(s_wt, nW + (1 if k == 0 else 0))
                            act.activation(WT[:, :, :], pT[:, 0:nW, :], ACT.Copy).then_inc(s_wc, 1)
                        if k == 0:
                            act.activation(xT[:, 0, 0:REL], pT[:, 3, 0:REL], ACT.Copy).then_inc(s_wc, 1)

                    @block.vector
                    def _(v):
                        n = [0]

                        def link(ins):
                            n[0] += 1
                            ins.then_inc(s_link, 1)
                            v.wait_ge(s_link, n[0])

                        if k == 0:
                            link(v.memset(B[:, N // P, :], 0.0))
                            link(v.memset(acc[:, :, :], 0.0))
                            v.wait_ge(s_rel, 1)
                            link(v.tensor_copy(relx[:, 0, :], pT[0:REL, 4, :]))
                            link(v.tensor_tensor(W1[0:REL, 4, :], pT[0:REL, 4, :], relx[:, 0, :], ALU.subtract))
                            link(v.tensor_copy(relx[:, 1, :], W1[0:REL, 4, :]))
                            link(v.tensor_tensor(relx[:, 2, :], W1[0:REL, 4, :], relx[:, 1, :], ALU.subtract))

                s_link2 = sem(f"s_link2{k}", c)
                LINKS = [13, 0, 0, 0, 0]
                LINKS = {}

                def vector_steps(v, i, per, final):
                    n = [0]
                    asked = [0]
                    ROOTS = {0: 0, 1: 2, 2: 2, 3: 1, 4: 1}[k]

                    def link(ins):
                        n[0] += 1
                        ins.then_inc(s_link2, 1)
                        v.wait_ge(s_link2, i * per + n[0])

                    T = bass.ds(i * G7, G7)
                    Bt = B[:, T, :]
                    At = acc[:, T, 0:P]

                    def bc(ap, n3=P):
                        return ap.unsqueeze(2).broadcast_to([P, G7, n3])

                    def heads(ap):
                        return ap.rearrange("p t (h d) -> p t h d", h=HEADS)

                    def bch(ap):
                        return ap.unsqueeze(3).broadcast_to([P, G7, HEADS, DV])

                    def bv(j):
                        return vec[:, j, :].unsqueeze(1).broadcast_to([P, G7, P])

                    def root():
                        asked[0] += 1
                        v.wait_ge(s_sqrt, i * ROOTS + asked[0])

                    def norm_heads(src):
                        apart(v)
                        link(v.tensor_reduce(m4[:, :, :], heads(src), AX.X, ALU.add))
                        link(v.tensor_scalar(m4[:, :, :], m4[:, :, :], 1.0 / DV, None, ALU.mult))
                        link(v.tensor_tensor(heads(W1[:, :, :]), heads(src), bch(m4[:, :, :]), ALU.subtract))
                        link(v.tensor_tensor(xT[:, :, :], W1[:, :, :], W1[:, :, :], ALU.mult))
                        link(v.tensor_reduce(v4[:, :, :], heads(xT[:, :, :]), AX.X, ALU.add))
                        v.tensor_scalar(v4[:, :, :], v4[:, :, :], 1.0 / DV, 1e-9, ALU.mult, ALU.add).then_inc(s_ask, 1)
                        root()
                        link(v.reciprocal(m4[:, :, :], v4[:, :, :]))
                        link(v.tensor_tensor(heads(W1[:, :, :]), heads(W1[:, :, :]), bch(m4[:, :, :]), ALU.mult))

                    def split(dst, y):
                        link(v.tensor_scalar(dst[:, T, 0, :], y, 1.0, None, ALU.mult))
                        link(v.tensor_tensor(y, y, dst[:, T, 0, :], ALU.subtract))
                        link(v.tensor_scalar(dst[:, T, 1, :], y, 1.0, None, ALU.mult))
                        link(v.tensor_tensor(dst[:, T, 2, :], y, dst[:, T, 1, :], ALU.subtract))

                    if k == 1:
                        link(v.tensor_tensor(At, At, bc(deg_in[:, T]), ALU.mult))
                        link(v.tensor_tensor(Bt, Bt, At, ALU.add))
                    if k == 2:
                        link(v.tensor_scalar(v4[:, :, :], acc[:, T, P:XW], 1e-30, None, ALU.max))
                        link(v.reciprocal(v4[:, :, :], v4[:, :, :]))
                        link(v.tensor_tensor(heads(At), heads(At), bch(v4[:, :, :]), ALU.mult))
                        norm_heads(At)
                        link(v.tensor_tensor(W1[:, :, :], W1[:, :, :], bv(3), ALU.mult))
                        link(v.tensor_tensor(W1[:, :, :], W1[:, :, :], bv(4), ALU.add))
                        link(v.scalar_tensor_tensor(out=Bt, in0=W1[:, :, :], scalar=0.5, in1=Bt, op0=ALU.mult, op1=ALU.add))
                    if k == 3:
                        link(v.tensor_scalar(At, At, 0.0, None, ALU.max))
                        link(v.tensor_tensor(Bt, Bt, At, ALU.add))
                    if k == 4:
                        link(v.tensor_tensor(At, At, bc(deg_out[:, T]), ALU.mult))
                        link(v.tensor_tensor(Bt, Bt, At, ALU.add))
                    if k > 0:
                        apart(v)
                        for j in range(G7):
                            ins = v.bn_stats(st[:, j, :], B[:, bass.ds(i * G7 + j, 1), :].rearrange("p a d -> p (a d)"))
                        link(ins)
                        apart(v)
                        for j in range(G7):
                            ins = v.bn_aggr(mv[:, j, :], st[:, j, :])
                        ins.then_inc(s_ask, 1)
                        root()
                        link(v.reciprocal(sd[:, :], sd[:, :]))
                        link(v.tensor_tensor(Bt, Bt, mv[:, :, 0:1].broadcast_to([P, G7, P]), ALU.subtract))
                        link(v.tensor_tensor(Bt, Bt, bc(sd[:, :]), ALU.mult))
                    if k < 4:
                        link(v.tensor_scalar(W1[:, :, :], Bt, 1.0, None, ALU.mult))
                    v.sem_inc(s_new, 1)
                    if k == 4:
                        return n[0]
                    v.wait_ge(s_y, i + 1)
                    Y = [p[:, 0:G7, :] for p in pY]
                    y = W1[:, :, :]
                    if k == 0:
                        link(v.tensor_tensor(y, Y[0], bv(0), ALU.add))
                        split(X, y)
                        link(v.tensor_tensor(Bt, Bt, Y[1], ALU.add))
                        link(v.tensor_tensor(Bt, Bt, bv(1), ALU.add))
                    if k == 1:
                        link(v.tensor_tensor(y, Y[0], bv(0), ALU.add))
                        link(v.tensor_scalar(Xw[:, T, 0:P], y, 0.0, None, ALU.max))
                        link(v.tensor_tensor(y, Xw[:, T, 0:P], bv(2), ALU.mult))
                        link(v.tensor_reduce(m4[:, :, :], heads(y), AX.X, ALU.add))
                        link(v.scalar_tensor_tensor(out=Xw[:, T, P:XW], in0=m4[:, :, :], scalar=0.2, in1=m4[:, :, :], op0=ALU.mult, op1=ALU.max))
                        link(v.tensor_tensor(y, Y[1], bv(1), ALU.add))
                        link(v.tensor_scalar(y, y, 0.0, None, ALU.max))
                        norm_heads(y)
                        link(v.tensor_tensor(y, y, bv(3), ALU.mult))
                        link(v.tensor_tensor(y, y, bv(4), ALU.add))
                        link(v.scalar_tensor_tensor(out=Bt, in0=y, scalar=0.5, in1=Bt, op0=ALU.mult, op1=ALU.add))
                    if k == 2:
                        link(v.tensor_tensor(y, Y[0], bv(0), ALU.add))
                        split(X, y)
                        link(v.tensor_tensor(y, Y[1], bv(1), ALU.add))
                        split(X2, y)
                        link(v.tensor_tensor(At, Y[2], bv(2), ALU.add))
                    if k == 3:
                        link(v.tensor_tensor(y, Y[0], bv(0), ALU.add))
                        link(v.tensor_tensor(y, y, bc(deg_out[:, T]), ALU.mult))
                        link(v.tensor_scalar(At, y, 1.0, None, ALU.mult))
                        split(X, y)
                    v.sem_inc(s_done, 1)
                    return n[0]

                PER = {0: 8, 1: 24, 2: 29, 3: 14, 4: 6}[k]
                ROOTS = {0: 0, 1: 2, 2: 2, 3: 1, 4: 1}[k]
                NB = NT // G7

                with nc.Block() as block:
                    @block.vector
                    def _(v):
                        with v.Fori(0, NB) as i:
                            n = vector_steps(v, i, PER, False)
                        assert n == PER, (k, n)

                    @block.scalar
                    def _(act):
                        with act.Fori(0, NB) as i:
                            def root(r, which):
                                act.wait_ge(s_ask, i * ROOTS + r)
                                if which == "norm":
                                    act.activation(sd[:, :], mv[:, :, 1:2].rearrange("p t a -> p (t a)"), ACT.Sqrt, bias=eps[:, 0:1]).then_inc(s_sqrt, 1)
                                else:
                                    act.activation(v4[:, :, :], v4[:, :, :], ACT.Sqrt).then_inc(s_sqrt, 1)

                            if k == 2:
                                root(1, "heads")
                            if k > 0:
                                root(2 if k == 2 else 1, "norm")
                            if k < 4:
                                act.wait_ge(s_tp, i + 1)
                                act.activation(xT[:, :, :], pT[:, 0:G7, :], ACT.Copy).then_inc(s_xt, 1)
                            if k == 1:
                                root(2, "heads")

                    @block.tensor
                    def _(pe):
                        if k == 4:
                            return
                        with pe.Fori(0, NB) as i:
                            pe.wait_ge(s_new, i + 1)
                            for j in range(G7):
                                tr = pe.transpose(pT[:, j, :], W1[:, j, :], ident_f[:, :])
                            tr.then_inc(s_tp, 1)
                            pe.wait_ge(s_xt, i + 1)
                            for w in range(nW):
                                for j in range(G7):
                                    mm = pe.matmul(pY[w][:, j, :], xT[:, j, :], WT[:, w, :], start=True, stop=True)
                            mm.then_inc(s_y, 1)

                    @block.sync
                    def _(sp):
                        if k == 4:
                            full = N // P
                            sp.wait_ge(s_new, NB)
                            sp.dma_start(out[0:full * P, :].rearrange("(t p) d -> p t d", p=P), B[:, 0:full, :]).then_inc(s_out, 16)
                            sp.dma_start(out[full * P:N, :], B[0:N - full * P, full, :]).then_inc(s_out, 16)
                            sp.wait_ge(s_out, 32)

                if k == 1:
                    s_gm = sem("s_gm", c)
                    s_gp = sem("s_gp", c)
                    s_e = sem("s_e", c)
                    s_ex = sem("s_ex", c)
                    q = Xw[:, :, P:XW]
                    with nc.Block() as block:
                        @block.vector
                        def _(v):
                            v.memset(acc[:, :, :], 0.0)
                            v.tensor_reduce(gm[:, 0, :], q.rearrange("p t h -> p h t"), AX.X, ALU.max).then_inc(s_gm, 1)
                            v.wait_ge(s_gp, 1)
                            v.tensor_tensor(q, q, gm[:, 1, :].unsqueeze(1).broadcast_to([P, NT, HEADS]), ALU.subtract).then_inc(s_e, 1)
                            v.wait_ge(s_ex, 1)
                            h = Xw[:, :, 0:P].rearrange("p t (h d) -> p t h d", h=HEADS)
                            v.tensor_tensor(h, h, q.unsqueeze(3).broadcast_to([P, NT, HEADS, DV]), ALU.mult).then_inc(s_e, 1)

                        @block.gpsimd
                        def _(gp):
                            gp.wait_ge(s_gm, 1)
                            gp.partition_all_reduce(gm[:, 1, :], gm[:, 0, :], P, RMAX).then_inc(s_gp, 1)

                        @block.scalar
                        def _(act):
                            act.wait_ge(s_e, 1)
                            act.activation(q, q, ACT.Exp).then_inc(s_ex, 1)

        node_stage(0)
        aggregate("relation", "0")
        node_stage(1)
        aggregate("weighted", "1")
        X2 = sb("X2", [P, NT, 3, P], BF16)
        node_stage(2)
        aggregate("typed", "2")
        node_stage(3)
        aggregate("plain", "3")
        node_stage(4)


_INS = ["x", "src", "dst", "edge_type_2", "edge_type_64", "edge_weight",
        "L0_gnn_W_self", "L0_gnn_b_self", "L0_gnn_W_msg", "L0_gnn_b_msg", "L0_gnn_rel_emb",
        "L1_gnn_W0", "L1_gnn_b0", "L1_gnn_W1", "L1_gnn_b1", "L1_gnn_attention", "L1_gnn_scale", "L1_gnn_offset",
        "L2_gnn_W_data", "L2_gnn_b_data", "L2_gnn_W_control", "L2_gnn_b_control", "L2_gnn_W_self", "L2_gnn_b_self",
        "L3_gnn_W", "L3_gnn_b"]


def kernel(**inputs):
    import numpy as _np
    import concourse.bacc as _bacc
    from concourse import mybir as _mybir
    from concourse.bass_utils import run_bass_kernel_spmd as _run

    nc = _bacc.Bacc("TRN2", target_bir_lowering=False, num_devices=1)
    arrays, args = {}, {}
    for name in _INS:
        a = _np.ascontiguousarray(inputs[name])
        arrays[f"in_{name}"] = a
        args[name] = nc.dram_tensor(f"in_{name}", a.shape, _mybir.dt.from_np(a.dtype), kind="ExternalInput").ap()
    out = nc.dram_tensor("out_0", inputs["x"].shape, _mybir.dt.float32, kind="ExternalOutput").ap()
    gnn_four_layers_kernel(nc, args, out)
    r = _run(nc, [arrays], core_ids=[0])
    return r.results[0]["out_0"]
```

```python
import concourse.bass as bass
from concourse import mybir
from contextlib import ExitStack

P = 128
ALU = mybir.AluOpType
ACT = mybir.ActivationFunctionType
AX = mybir.AxisListType
F32 = mybir.dt.float32
BF16 = mybir.dt.bfloat16
I32 = mybir.dt.int32
U32 = mybir.dt.uint32
U8 = mybir.dt.uint8
RMAX = bass.bass_isa.ReduceOp.max

QUAD = 4
GROUP = 16
PAIR = 4
HEADS = 4
XW = 132
REC = 16
F_SL, F_W = 0, 1
H_DL, H_SL2, H_REL = 4, 5, 6
B_TS, B_TD = 14, 15


def gnn_four_layers_kernel(nc, t, out):
    N, D = t["x"].shape
    E = t["src"].shape[0]
    REL = t["L0_gnn_rel_emb"].shape[0]
    NT = -(-N // P)
    COLS = -(-(-(-E // P)) // (2 * GROUP)) * 2 * GROUP
    SLOTS = P * COLS
    PAD = NT * P - 1
    BUCKETS = NT * NT
    NOV = -(-(SLOTS // P) // (2 * PAIR)) * 2 * PAIR
    NREC = BUCKETS + NOV
    assert D == P and N < NT * P and NT < 64 and REL <= 64

    rec_d = nc.dram_tensor("records", (P * NREC, REC // 4), F32, kind="Internal").ap()

    with ExitStack() as ctx:
        def sb(name, shape, dt, c=ctx):
            return c.enter_context(nc.sbuf_tensor(name, shape, dt))

        def sem(name, c=ctx):
            return c.enter_context(nc.semaphore(name))

        def ps(name, shape, c, dt=F32):
            return c.enter_context(nc.psum_tensor(name, shape, dt))

        passed = sem("passed")

        def apart(eng):
            eng.sem_inc(passed, 1)

        iota_f = sb("iota_f", [P, P], F32)
        iota_b = sb("iota_b", [P, 2 * P], BF16)
        ident_f = sb("ident_f", [P, P], F32)
        ident_b = sb("ident_b", [P, P], BF16)
        zero_b = sb("zero_b", [P, P], BF16)
        eps = sb("eps", [P, 2], F32)
        deg_out = sb("deg_out", [P, NT], F32)
        deg_in = sb("deg_in", [P, NT], F32)
        n_over = sb("n_over", [1, 1], I32)

        with ExitStack() as c1:
            ones_f = sb("ones_f", [P, P], F32, c1)
            before = sb("before", [P, P], F32, c1)
            after = sb("after", [P, P], F32, c1)
            esrc = sb("esrc", [P, COLS], I32, c1)
            edst = sb("edst", [P, COLS], I32, c1)
            ety2 = sb("ety2", [P, COLS], I32, c1)
            ety64 = sb("ety64", [P, COLS], I32, c1)
            ew = sb("ew", [P, COLS], F32, c1)
            tmp = sb("tmp", [P, COLS], I32, c1)
            ts_b = sb("ts_b", [P, COLS + GROUP], BF16, c1)
            td_b = sb("td_b", [P, COLS + GROUP], BF16, c1)
            sl_b = sb("sl_b", [P, COLS], BF16, c1)
            ts64_b = sb("ts64_b", [P, COLS + GROUP], BF16, c1)
            own = sb("own", [P, COLS], F32, c1)
            bucket = sb("bucket", [NT, NT], F32, c1)
            key = sb("key", [P, COLS + GROUP], F32, c1)
            rec = sb("rec", [P, COLS, REC // 4], F32, c1)
            null = sb("null", [P, 8 * GROUP, REC // 4], F32, c1)
            run = sb("run", [NT, 2, QUAD, 2, NT], F32, c1)
            rec_h = rec[:, :, :].bitcast(BF16)
            rec_8 = rec[:, :, :].bitcast(U8)
            null_h = null[:, :, :].bitcast(BF16)
            null_8 = null[:, :, :].bitcast(U8)

            loads = sem("loads", c1)
            pads = sem("pads", c1)
            consts = sem("consts", c1)
            pool_step = sem("pool_step", c1)
            prep = sem("prep", c1)
            null_ok = sem("null_ok", c1)
            nulled = sem("nulled", c1)

            with nc.Block() as block:
                full = E // COLS
                rest = E - full * COLS

                @block.sync
                def _(sp):
                    sp.wait_ge(pads, 5)
                    for tl, name in ((esrc, "src"), (edst, "dst"), (ety2, "edge_type_2"),
                                     (ety64, "edge_type_64"), (ew, "edge_weight")):
                        sp.dma_start(tl[0:full, :], t[name][0:full * COLS].rearrange("(p c) -> p c", c=COLS)).then_inc(loads, 16)
                        if rest:
                            sp.dma_start(tl[full:full + 1, 0:rest], t[name][full * COLS:E].rearrange("(p c) -> p c", p=1)).then_inc(loads, 16)
                    sp.wait_ge(null_ok, 4)
                    r = rec_d.rearrange("(p c) w -> p (c w)", p=P)
                    W = REC // 4
                    step = 8 * GROUP
                    n = 0
                    for a in range(0, NREC, step):
                        b = min(a + step, NREC)
                        sp.dma_start(r[:, a * W:b * W], null[:, 0:b - a, :].rearrange("p c w -> p (c w)")).then_inc(nulled, 16)
                        n += 16
                    sp.wait_ge(nulled, n)

                @block.gpsimd
                def _(gp):
                    gp.iota(iota_f[:, :], pattern=[[1, P]], base=0, channel_multiplier=0,
                            allow_small_or_imprecise_dtypes=True).then_inc(consts, 1)
                    gp.iota(iota_b[:, :], pattern=[[1, 2 * P]], base=0, channel_multiplier=0,
                            allow_small_or_imprecise_dtypes=True).then_inc(consts, 1)
                    gp.iota(bucket[:, :], pattern=[[1, NT]], base=0, channel_multiplier=NT,
                            allow_small_or_imprecise_dtypes=True).then_inc(consts, 1)
                    for m, v in ((ident_f, 0.0), (ident_b, 0.0), (before, 1.0), (after, 1.0)):
                        gp.memset(m[:, :], v).then_inc(pool_step, 1)
                    gp.memset(ones_f[:, :], 1.0).then_inc(consts, 1)
                    gp.memset(zero_b[:, :], 0.0).then_inc(consts, 1)
                    gp.memset(eps[:, 0:1], 1e-5).then_inc(consts, 1)
                    gp.memset(eps[:, 1:2], 1e-9).then_inc(consts, 1)
                    gp.wait_ge(pool_step, 4)
                    for m in (ident_f, ident_b):
                        gp.affine_select(out=m[:, :], in_=m[:, :], compare_op=ALU.not_equal, fill=1.0,
                                         base=0, pattern=[[-1, P]], channel_multiplier=1).then_inc(consts, 1)
                    gp.affine_select(out=before[:, :], in_=before[:, :], compare_op=ALU.is_gt, fill=0.0,
                                     base=0, pattern=[[-1, P]], channel_multiplier=1).then_inc(consts, 1)
                    gp.affine_select(out=after[:, :], in_=after[:, :], compare_op=ALU.is_gt, fill=0.0,
                                     base=0, pattern=[[1, P]], channel_multiplier=-1).then_inc(consts, 1)

                @block.vector
                def _(v):
                    n = [0]

                    def link(ins):
                        n[0] += 1
                        ins.then_inc(prep, 1)
                        v.wait_ge(prep, n[0])

                    v.memset(esrc[:, :], PAD).then_inc(pads, 1)
                    v.memset(edst[:, :], PAD).then_inc(pads, 1)
                    v.memset(ety2[:, :], 0).then_inc(pads, 1)
                    v.memset(ety64[:, :], 0).then_inc(pads, 1)
                    v.memset(ew[:, :], 0.0).then_inc(pads, 1)
                    link(v.memset(null[:, :, :], 0.0))
                    v.memset(null[:, :, F_SL:F_SL + 1], -1.0).then_inc(null_ok, 1)
                    v.memset(null_h[:, :, H_DL:H_DL + 1], -1.0).then_inc(null_ok, 1)
                    v.memset(null_h[:, :, H_SL2:H_SL2 + 1], -1.0).then_inc(null_ok, 1)
                    v.memset(null_h[:, :, H_REL:H_REL + 1], -1.0).then_inc(null_ok, 1)
                    v.wait_ge(loads, 16 * 5 * (2 if rest else 1))
                    link(v.tensor_scalar(tmp[:, :], esrc[:, :], 7, None, ALU.logical_shift_right))
                    for a in (ts_b, td_b, ts64_b, key):
                        link(v.memset(a[:, COLS:COLS + GROUP], 0.0))
                    link(v.tensor_copy(ts_b[:, 0:COLS], tmp[:, :]))
                    link(v.tensor_copy(rec_8[:, :, B_TS], tmp[:, :]))
                    link(v.tensor_scalar(key[:, 0:COLS], tmp[:, :], 64.0, None, ALU.mult))
                    link(v.tensor_copy(ts64_b[:, 0:COLS], key[:, 0:COLS]))
                    link(v.tensor_scalar(own[:, :], tmp[:, :], float(NT), None, ALU.mult))
                    link(v.tensor_scalar(tmp[:, :], edst[:, :], 7, None, ALU.logical_shift_right))
                    link(v.tensor_copy(td_b[:, 0:COLS], tmp[:, :]))
                    link(v.tensor_copy(rec_8[:, :, B_TD], tmp[:, :]))
                    link(v.tensor_tensor(key[:, 0:COLS], key[:, 0:COLS], tmp[:, :], ALU.add))
                    link(v.tensor_tensor(own[:, :], own[:, :], tmp[:, :], ALU.add))
                    link(v.tensor_scalar(own[:, :], own[:, :], float(P), None, ALU.mult))
                    link(v.tensor_scalar(tmp[:, :], edst[:, :], P - 1, None, ALU.bitwise_and))
                    link(v.tensor_copy(rec_h[:, :, H_DL], tmp[:, :]))
                    link(v.tensor_scalar(tmp[:, :], esrc[:, :], P - 1, None, ALU.bitwise_and))
                    link(v.tensor_copy(rec[:, :, F_SL], tmp[:, :]))
                    link(v.tensor_copy(sl_b[:, :], tmp[:, :]))
                    link(v.tensor_copy(rec[:, :, F_W], ew[:, :]))
                    link(v.tensor_scalar(ety2[:, :], ety2[:, :], 0.0, float(P), ALU.not_equal, ALU.mult))
                    link(v.tensor_tensor(rec_h[:, :, H_SL2], ety2[:, :], tmp[:, :], ALU.add))
                    link(v.tensor_scalar(rec_h[:, :, H_REL], ety64[:, :], 0.0, float(REL - 1), ALU.max, ALU.min))
                    v.wait_ge(consts, 11)

            with ExitStack() as c2:
                pH = ps("pH", [NT, 512], c2)
                pOut = ps("pOut", [NT, 512], c2)
                pIn = ps("pIn", [NT, 512], c2)
                pB = ps("pB", [P, 512], c2)
                pD = ps("pD", [P, 512], c2)
                hts = sb("hts", [P, 2, GROUP, NT], BF16, c2)
                htd = sb("htd", [P, 2, GROUP, NT], BF16, c2)
                hsl = sb("hsl", [P, 2, GROUP, P], BF16, c2)
                hdl = sb("hdl", [P, 2, GROUP, P], BF16, c2)
                cnt = sb("cnt", [NT, NT], F32, c2)
                cnti = sb("cnti", [NT, NT], I32, c2)
                incl = sb("incl", [NT, NT], F32, c2)
                dego = sb("dego", [NT, P], F32, c2)
                degi = sb("degi", [NT, P], F32, c2)
                degs = sb("degs", [P, 2, NT], F32, c2)
                hot = sem("hot", c2)
                counted = sem("counted", c2)
                ostep = sem("ostep", c2)
                tri_done = sem("tri_done", c2)
                deg_t = sem("deg_t", c2)
                sq = sem("sq", c2)
                HN = COLS // (2 * GROUP)
                with nc.Block() as block:
                    @block.vector
                    def _(v):
                        def onehots(g_first, par):
                            cols = bass.ds(g_first, GROUP)
                            for o, src, w in ((hts, ts_b, NT), (htd, td_b, NT), (hsl, sl_b, P), (hdl, None, P)):
                                s = (rec_h[:, cols, H_DL] if src is None else src[:, cols])
                                ins = v.tensor_tensor(o[:, par, :, :], iota_b[:, 0:w].unsqueeze(1).broadcast_to([P, GROUP, w]),
                                                      s.unsqueeze(2).broadcast_to([P, GROUP, w]), ALU.is_equal)
                            ins.then_inc(hot, 1)

                        with v.Fori(0, HN) as i:
                            for par in range(2):
                                v.wait_ge(counted, 2 * i + par + 1)
                                onehots(i * 2 * GROUP + par * GROUP, par)
                        v.wait_ge(counted, 2 * HN + 3)
                        n = [0]

                        def link(ins):
                            n[0] += 1
                            ins.then_inc(ostep, 1)
                            v.wait_ge(ostep, n[0])

                        link(v.tensor_scalar(cnti[:, :], pH[:, 0:NT], float(P - 1), None, ALU.add))
                        link(v.tensor_scalar(cnti[:, :], cnti[:, :], 7, None, ALU.logical_shift_right))
                        link(v.tensor_scalar(cnt[:, :], cnti[:, :], -1.0, 0.0, ALU.add, ALU.max))
                        link(v.tensor_tensor_scan(incl[:, :], ones_f[0:NT, 0:NT], cnt[:, :], 0.0, ALU.mult, ALU.add))
                        link(v.tensor_tensor(cnt[:, :], incl[:, :], cnt[:, :], ALU.subtract))
                        link(v.tensor_copy(dego[:, :], pOut[:, 0:P]))
                        link(v.tensor_copy(degi[:, :], pIn[:, 0:P]))
                        link(v.tensor_tensor(cnt[:, :], cnt[:, :], bucket[:, :], ALU.subtract))
                        v.wait_ge(tri_done, 2)
                        link(v.tensor_scalar(cnt[:, :], cnt[:, :], pB[0:NT, 0:1], float(BUCKETS - 1), ALU.add, ALU.add))
                        link(v.tensor_scalar(run[:, :, :, 1, :].rearrange("p a b n -> p (a b) n"), cnt[:, :].unsqueeze(1).broadcast_to([NT, 2 * QUAD, NT]),
                                             float(P), None, ALU.mult))
                        link(v.tensor_copy(n_over[:, :], pB[0:1, 8:9]))
                        v.wait_ge(deg_t, 2)
                        link(v.tensor_scalar(degs[:, 0, :], pD[:, 128:128 + NT], 1.0, None, ALU.add))
                        link(v.tensor_scalar(degs[:, 1, :], pD[:, 256:256 + NT], 1.0, None, ALU.max))
                        link(v.reciprocal(deg_in[:, :], degs[:, 1, :]))
                        v.wait_ge(sq, 1)
                        link(v.reciprocal(deg_out[:, :], degs[:, 0, :]))

                    @block.tensor
                    def _(pe):
                        pe.matmul(pH[:, 0:NT], zero_b[:, 0:NT], zero_b[:, 0:NT], start=True, stop=False, skip_group_check=True)
                        pe.matmul(pOut[:, 0:P], zero_b[:, 0:NT], zero_b[:, 0:P], start=True, stop=False, skip_group_check=True)
                        pe.matmul(pIn[:, 0:P], zero_b[:, 0:NT], zero_b[:, 0:P], start=True, stop=False, skip_group_check=True).then_inc(counted, 2)
                        with pe.Fori(0, HN) as i:
                            for par in range(2):
                                pe.wait_ge(hot, 2 * i + par + 1)
                                for k in range(GROUP):
                                    pe.matmul(pH[:, 0:NT], hts[:, par, k, :], htd[:, par, k, :], start=False, stop=False, skip_group_check=True)
                                    pe.matmul(pOut[:, 0:P], hts[:, par, k, :], hsl[:, par, k, :], start=False, stop=False, skip_group_check=True)
                                    mm = pe.matmul(pIn[:, 0:P], htd[:, par, k, :], hdl[:, par, k, :], start=False, stop=False, skip_group_check=True)
                                mm.then_inc(counted, 1)
                        pe.matmul(pH[:, 0:NT], zero_b[:, 0:NT], zero_b[:, 0:NT], start=False, stop=True, skip_group_check=True)
                        pe.matmul(pOut[:, 0:P], zero_b[:, 0:NT], zero_b[:, 0:P], start=False, stop=True, skip_group_check=True)
                        pe.matmul(pIn[:, 0:P], zero_b[:, 0:NT], zero_b[:, 0:P], start=False, stop=True, skip_group_check=True).then_inc(counted, 1)
                        pe.wait_ge(ostep, 7)
                        pe.matmul(pB[0:NT, 0:1], after[0:NT, 0:NT], incl[:, NT - 1:NT], start=True, stop=True).then_inc(tri_done, 1)
                        pe.matmul(pB[0:1, 8:9], incl[:, NT - 1:NT], ones_f[0:NT, 0:1], start=True, stop=True).then_inc(tri_done, 1)
                        pe.transpose(pD[:, 128:128 + NT], dego[:, :], ident_f[0:NT, 0:NT]).then_inc(deg_t, 1)
                        pe.transpose(pD[:, 256:256 + NT], degi[:, :], ident_f[0:NT, 0:NT]).then_inc(deg_t, 1)

                    @block.scalar
                    def _(act):
                        act.wait_ge(ostep, 12)
                        act.activation(degs[:, 0, :], degs[:, 0, :], ACT.Sqrt).then_inc(sq, 1)

            with ExitStack() as c2:
                hts = sb("hts2", [P, 2, GROUP, NT], BF16, c2)
                htd = sb("htd2", [P, 2, GROUP, NT], BF16, c2)
                hT = sb("hT", [NT, 2, QUAD, P], F32, c2)
                junk = sb("junk", [P, 2, QUAD, P], F32, c2)
                prod = sb("prod", [P, GROUP, 2, NT], F32, c2)
                rank = sb("rank", [P, 2, GROUP], F32, c2)
                base = sb("base", [P, GROUP, 2], F32, c2)
                far = sb("far", [P, GROUP], F32, c2)
                pos = sb("pos", [P, GROUP], I32, c2)
                posl = sb("posl", [P, GROUP], I32, c2)
                posh = sb("posh", [P, GROUP], I32, c2)
                idx = sb("idx", [P, 2, GROUP], U32, c2)
                ring = sb("ring", [P, 2, GROUP, REC // 4], F32, c2)
                pK = [ps(f"pK{i}", [P, 512], c2) for i in range(2)]
                pT = [ps(f"pT{i}", [P, 512], c2) for i in range(2)]
                pG = [ps(f"pG{i}", [P, 512], c2) for i in range(2)]
                pR = ps("pR", [P, 512], c2)

                DEPTH = 2
                s_hot = sem("s_hot", c2)
                s_hot_free = sem("s_hot_free", c2)
                s_krow = sem("s_krow", c2)
                s_tr = sem("s_tr", c2)
                s_ht = sem("s_ht", c2)
                s_run = sem("s_run", c2)
                s_look = sem("s_look", c2)
                s_add = sem("s_add", c2)
                s_rank = sem("s_rank", c2)
                s_base = sem("s_base", c2)
                s_pos = sem("s_pos", c2)
                s_idx = sem("s_idx", c2)
                s_ring = sem("s_ring", c2)
                s_sent = [sem(f"s_sent{i}", c2) for i in range(2)]
                NG2 = COLS // (2 * GROUP)

                with nc.Block() as block:
                    @block.vector
                    def _(v):
                        v.sem_inc(s_rank, DEPTH)
                        v.sem_inc(s_base, DEPTH)

                        def hot(g, par):
                            v.wait_ge(s_hot_free, g + 1)
                            for o, src in ((hts, ts_b), (htd, td_b)):
                                ins = v.tensor_tensor(o[:, par, :, :], iota_b[:, 0:NT].unsqueeze(1).broadcast_to([P, GROUP, NT]),
                                                      src[:, bass.ds(g * GROUP, GROUP)].unsqueeze(2).broadcast_to([P, GROUP, NT]), ALU.is_equal)
                            ins.then_inc(s_hot, 1)

                        hot(0, 0)
                        with v.Fori(0, NG2) as i:
                            for par in range(2):
                                g = 2 * i + par
                                for w in range(GROUP // QUAD):
                                    q = g * (GROUP // QUAD) + w
                                    v.wait_ge(s_krow, q + 3)
                                    for k in range(QUAD):
                                        col = w * QUAD + k
                                        ins = v.scalar_tensor_tensor(out=junk[:, w % 2, k, :], in0=pK[w % 2][:, k * P:(k + 1) * P], scalar=key[:, bass.ds(g * GROUP + col, 1)],
                                                                     in1=before[:, :], op0=ALU.is_equal, op1=ALU.mult, accum_out=rank[:, par, col:col + 1])
                                    ins.then_inc(s_rank, 1)
                                    v.wait_ge(s_look, q + 3)
                                    v.tensor_tensor(prod[:, w * QUAD:(w + 1) * QUAD, :, :], pG[w % 2][:, 0:QUAD * 2 * NT].rearrange("p (k a b) -> p k a b", k=QUAD, a=2),
                                                    htd[:, par, w * QUAD:(w + 1) * QUAD, :].unsqueeze(2).broadcast_to([P, QUAD, 2, NT]), ALU.mult).then_inc(s_base, 1)
                                    if w == 1:
                                        hot(g + 1, 1 - par)
                                v.wait_ge(s_base, (g + 1) * (GROUP // QUAD) + 2)
                                v.tensor_reduce(base[:, :, :], prod[:, :, :, :], AX.X, ALU.add).then_inc(s_pos, 1)
                                v.wait_ge(s_pos, g * 8 + 1)
                                v.tensor_tensor(base[:, :, 0], rank[:, par, :], base[:, :, 0], ALU.add).then_inc(s_pos, 1)
                                v.wait_ge(s_pos, g * 8 + 2)
                                v.scalar_tensor_tensor(out=far[:, :], in0=base[:, :, 0], scalar=float(P), in1=base[:, :, 1],
                                                       op0=ALU.is_ge, op1=ALU.mult).then_inc(s_pos, 1)
                                v.wait_ge(s_pos, g * 8 + 3)
                                v.tensor_tensor(far[:, :], far[:, :], base[:, :, 0], ALU.add).then_inc(s_pos, 1)
                                v.wait_ge(s_pos, g * 8 + 4)
                                v.tensor_tensor(pos[:, :], far[:, :], own[:, bass.ds(g * GROUP, GROUP)], ALU.add).then_inc(s_pos, 1)
                                v.wait_ge(s_pos, g * 8 + 5)
                                v.tensor_scalar(posl[:, :], pos[:, :], P - 1, None, ALU.bitwise_and).then_inc(s_pos, 1)
                                v.tensor_scalar(posh[:, :], pos[:, :], 7, None, ALU.logical_shift_right).then_inc(s_pos, 1)
                                v.wait_ge(s_pos, g * 8 + 7)
                                v.wait_ge(s_sent[par], i * (16 * GROUP) + 16)
                                v.scalar_tensor_tensor(out=idx[:, par, :], in0=posl[:, :], scalar=float(NREC), in1=posh[:, :],
                                                       op0=ALU.mult, op1=ALU.add).then_inc(s_idx, 1)
                                v.sem_inc(s_pos, 1)

                    @block.tensor
                    def _(pe):
                        pe.sem_inc(s_hot_free, DEPTH)
                        pe.sem_inc(s_krow, DEPTH)
                        pe.sem_inc(s_tr, DEPTH)
                        pe.sem_inc(s_look, DEPTH)
                        pe.matmul(pR[0:NT, 0:NT], zero_b[:, 0:NT], zero_b[:, 0:NT], start=True, stop=False, skip_group_check=True).then_inc(s_add, 1)

                        def keys_and_turn(q, w, par, g):
                            pe.wait_ge(s_rank, q + 1)
                            for k in range(QUAD):
                                col = g * GROUP + w * QUAD + k
                                for part, st in ((ts64_b, True), (td_b, False)):
                                    mm = pe.matmul(pK[w % 2][:, k * P:(k + 1) * P], part[:, bass.ds(col, 1)].broadcast_to([P, P]), ident_b[:, :], start=st, stop=not st)
                            mm.then_inc(s_krow, 1)
                            pe.wait_ge(s_ht, q + 1)
                            for k in range(QUAD):
                                mm = pe.matmul(pT[w % 2][0:NT, k * P:(k + 1) * P], hts[:, par, w * QUAD + k, :], ident_b[:, :], start=True, stop=True)
                            mm.then_inc(s_tr, 1)

                        pe.wait_ge(s_hot, 1)
                        keys_and_turn(0, 0, 0, 0)
                        with pe.Fori(0, NG2) as i:
                            for par in range(2):
                                g = 2 * i + par
                                for w in range(GROUP // QUAD):
                                    q = g * (GROUP // QUAD) + w
                                    for k in range(QUAD):
                                        pe.wait_ge(s_run, q * QUAD + k + 1)
                                        pe.matmul(pR[0:NT, 0:NT], hts[:, par, w * QUAD + k, :], htd[:, par, w * QUAD + k, :], start=False, stop=False, skip_group_check=True).then_inc(s_add, 1)
                                    if w + 1 < GROUP // QUAD:
                                        keys_and_turn(q + 1, w + 1, par, g)
                                    else:
                                        pe.wait_ge(s_hot, g + 2)
                                        keys_and_turn(q + 1, 0, 1 - par, g + 1)
                                    pe.wait_ge(s_ht, q + 3)
                                    pe.wait_ge(s_base, q + 1)
                                    for k in range(QUAD):
                                        mm = pe.matmul(pG[w % 2][:, k * 2 * NT:(k + 1) * 2 * NT], hT[:, w % 2, k, :], run[:, w % 2, k, :, :].rearrange("p a b -> p (a b)"), start=True, stop=True)
                                    mm.then_inc(s_look, 1)
                                pe.wait_ge(s_add, g * GROUP + GROUP + 1)
                                pe.sem_inc(s_hot_free, 1)
                        pe.matmul(pR[0:NT, 0:NT], zero_b[:, 0:NT], zero_b[:, 0:NT], start=False, stop=True, skip_group_check=True)

                    @block.scalar
                    def _(act):
                        act.sem_inc(s_ht, DEPTH)

                        def turned(q, w):
                            act.wait_ge(s_tr, q + 3)
                            act.wait_ge(s_look, q + 1)
                            act.activation(hT[:, w % 2, :, :].rearrange("p k n -> p (k n)"), pT[w % 2][0:NT, 0:QUAD * P], ACT.Copy).then_inc(s_ht, 1)

                        turned(0, 0)
                        with act.Fori(0, NG2) as i:
                            for par in range(2):
                                g = 2 * i + par
                                for w in range(GROUP // QUAD):
                                    q = g * (GROUP // QUAD) + w
                                    act.wait_ge(s_look, q + 1)
                                    for k in range(QUAD):
                                        act.wait_ge(s_add, q * QUAD + k + 1)
                                        act.activation(run[:, w % 2, k, 0, :], pR[0:NT, 0:NT], ACT.Copy).then_inc(s_run, 1)
                                    turned(q + 1, w + 1)
                                act.wait_ge(s_sent[par], i * (16 * GROUP) + 16)
                                apart(act)
                                act.copy(ring[:, par, :, :].rearrange("p c w -> p (c w)").bitcast(I32),
                                         rec[:, bass.ds(g * GROUP, GROUP), :].rearrange("p c w -> p (c w)").bitcast(I32)).then_inc(s_ring, 1)

                    @block.gpsimd
                    def _(gp):
                        for par in range(2):
                            gp.dma_start(rec_d[NREC - 1 - par:NREC - par, :], null[0:1, 0, :]).then_inc(s_sent[par], 16)
                        with gp.Fori(0, NG2) as i:
                            for par in range(2):
                                g = 2 * i + par
                                gp.wait_ge(s_idx, g + 1)
                                gp.wait_ge(s_ring, g + 1)
                                apart(gp)
                                for k in range(GROUP):
                                    gp.indirect_dma_start(rec_d, bass.IndirectOffsetOnAxis(ap=idx[:, par, k:k + 1], axis=0),
                                                          ring[:, par, k, :], None).then_inc(s_sent[par], 16)
                        gp.wait_ge(s_sent[0], NG2 * 16 * GROUP + 16)
                        gp.wait_ge(s_sent[1], NG2 * 16 * GROUP + 16)

        recs = sb("recs", [P, NREC, REC // 4], F32)
        recs_h = recs[:, :, :].bitcast(BF16)
        recs_8 = recs[:, :, :].bitcast(U8)
        relx = sb("relx", [REL, 3, P], BF16)
        B = sb("B", [P, NT, P], F32)
        acc = sb("acc", [P, NT, XW], F32)
        X = sb("X", [P, NT, 3, P], BF16)
        tiles = sb("tiles", [1, NOV, 2], U8)
        relw = sb("relw", [REL, P], F32)
        with ExitStack() as c1:
            s_recs = sem("s_recs", c1)
            s_tiles = sem("s_tiles", c1)
            with nc.Block() as block:
                @block.sync
                def _(sp):
                    sp.dma_start(recs[:, :, :].rearrange("p c w -> p (c w)"), rec_d.rearrange("(p c) w -> p (c w)", p=P)).then_inc(s_recs, 16)

                @block.vector
                def _(v):
                    v.wait_ge(s_recs, 16)
                    v.tensor_copy(tiles[:, :, :], recs_8[0:1, BUCKETS:NREC, B_TS:B_TD + 1]).then_inc(s_tiles, 1)
                    v.wait_ge(s_tiles, 1)

        def aggregate_own(mode, name):
            by_source = mode in ("relation", "typed")
            H = 2 if mode == "typed" else 1
            cdt = F32 if mode == "weighted" else BF16
            width = XW if mode == "weighted" else 3 * P
            NQ = 8
            cut = [NT * q // NQ for q in range(NQ + 1)]
            most = max(cut[q + 1] - cut[q] for q in range(NQ))
            NHB = 4 if mode == "relation" else 2
            iota = iota_f if mode == "weighted" else iota_b
            with ExitStack() as c:
                h1 = sb(f"g1{name}", [P, NHB, most, H * P], cdt, c)
                h2 = sb(f"g2{name}", [P, NHB, most, P], cdt, c)
                h3 = sb(f"g3{name}", [P, NHB, most, 64], BF16, c) if mode == "relation" else None
                Cs = sb(f"gC{name}", [P, 2, most, P], cdt, c)
                total = sb(f"total{name}", [P, P], F32, c)
                rel_t = sb(f"rel_t{name}", [REL, P], F32, c)
                pC = [ps(f"qC{name}{i}", [P, 8, P], c) for i in range(2)]
                pO = ps(f"qO{name}", [P, 512], c)
                pR = ps(f"qR{name}", [64, 512], c)
                pE = ps(f"qE{name}", [P, 512], c)
                PRE = 4
                U = NQ * H
                s_hot = sem(f"t_hot{name}", c)
                s_c = sem(f"t_c{name}", c)
                s_cs = sem(f"t_cs{name}", c)
                s_o = sem(f"t_o{name}", c)
                s_sum = sem(f"t_sum{name}", c)
                s_rel, s_relm = [sem(f"{n}{name}", c) if mode == "relation" else None for n in ("t_rel", "t_relm")]
                s_total = sem(f"t_total{name}", c) if mode != "weighted" else None
                s_taken = sem(f"t_taken{name}", c)

                with nc.Block() as block:
                    @block.vector
                    def _(v):
                        v.sem_inc(s_taken, 1)

                        def make(i, q):
                            Q = i * NQ + q
                            if mode == "relation":
                                v.wait_ge(s_o, Q - NHB + 1 + PRE)
                            else:
                                v.wait_ge(s_c, (Q - 1) * H + PRE)
                            b = i + q // NQ
                            q = q % NQ
                            par = q % NHB
                            n = cut[q + 1] - cut[q]

                            def same(o, f, w):
                                r = recs if f in (F_SL, F_W) else recs_h
                                own = bass.DynSlice(cut[q] * NT + b, n, NT) if by_source else bass.ds(b * NT + cut[q], n)
                                r = r[:, own, f].unsqueeze(2).broadcast_to([P, n, w])
                                return v.tensor_tensor(o, iota[:, 0:w].unsqueeze(1).broadcast_to([P, n, w]), r, ALU.is_equal)

                            same(h2[:, par, 0:n, :], H_DL, P)
                            if mode == "relation":
                                same(h3[:, par, 0:n, :], H_REL, 64)
                            if mode == "weighted":
                                for k in range(n):
                                    ch = b * NT + cut[q] + k
                                    f32 = recs[:, bass.ds(ch, 1), F_SL:F_W + 1].rearrange("p a w -> p (a w)")
                                    ins = v.tensor_scalar(h1[:, par, k, :], iota[:, 0:P], f32[:, 0:1], f32[:, 1:2], ALU.is_equal, ALU.mult)
                            elif mode == "typed":
                                ins = same(h1[:, par, 0:n, :], H_SL2, 2 * P)
                            else:
                                ins = same(h1[:, par, 0:n, :], F_SL, P)
                            ins.then_inc(s_hot, 1)

                        make(0, 0)
                        make(0, 1)
                        with v.Fori(0, NT) as i:
                            for q in range(NQ):
                                make(i, q + 2)
                            dst = acc[:, bass.ds(i, 1), 0:(XW if mode == "weighted" else P)].rearrange("p a w -> p (a w)")
                            v.wait_ge(s_sum, i + 1)
                            if mode == "weighted":
                                v.tensor_tensor(dst, dst, pO[:, 0:XW], ALU.add).then_inc(s_taken, 1)
                            else:
                                v.tensor_reduce(total[:, :], pO[:, 0:3 * P].rearrange("p (s d) -> p d s", s=3), AX.X, ALU.add).then_inc(s_total, 1)
                                if mode == "relation":
                                    v.wait_ge(s_relm, i + 1)
                                    v.wait_ge(s_total, 2 * i + 1)
                                    v.tensor_tensor(total[:, :], total[:, :], pE[:, 0:P], ALU.add).then_inc(s_total, 1)
                                    v.wait_ge(s_total, 2 * i + 2)
                                else:
                                    v.wait_ge(s_total, i + 1)
                                v.tensor_tensor(dst, dst, total[:, :], ALU.add).then_inc(s_taken, 1)

                    @block.scalar
                    def _(act):
                        act.sem_inc(s_cs, PRE)
                        with act.Fori(0, NT) as i:
                            for u in range(U):
                                n = cut[u // H + 1] - cut[u // H]
                                act.wait_ge(s_c, i * U + u + 1 + PRE)
                                act.wait_ge(s_o, i * U + u - 1 + PRE)
                                act.activation(Cs[:, u % 2, 0:n, :], pC[u % 2][:, 0:n, :], ACT.Copy).then_inc(s_cs, 1)
                            if mode == "relation":
                                act.wait_ge(s_sum, i + 1)
                                act.activation(rel_t[:, :], pR[0:REL, 0:P], ACT.Copy).then_inc(s_rel, 1)

                    @block.tensor
                    def _(pe):
                        pe.sem_inc(s_c, PRE)
                        pe.sem_inc(s_o, PRE)

                        def table(i, u):
                            G = i * U + u
                            if u % H == 0:
                                pe.wait_ge(s_hot, i * NQ + u // H + 1)
                            u = u % U
                            q, h = u // H, u % H
                            pe.wait_ge(s_cs, G - 1 + PRE)
                            for k in range(cut[q + 1] - cut[q]):
                                w1, w2 = h1[:, q % NHB, k, h * P:(h + 1) * P], h2[:, q % NHB, k, :]
                                lhsT, rhs = (w1, w2) if by_source else (w2, w1)
                                mm = pe.matmul(pC[u % 2][:, k, :], lhsT, rhs, start=True, stop=True)
                            mm.then_inc(s_c, 1)

                        table(0, 0)
                        with pe.Fori(0, NT) as i:
                            for u in range(U):
                                table(i, u + 1)
                                q, h = u // H, u % H
                                if u == 0:
                                    pe.wait_ge(s_taken, i + 1)
                                pe.wait_ge(s_cs, i * U + u + 1 + PRE)
                                for k in range(cut[q + 1] - cut[q]):
                                    a = cut[q] + k
                                    x = Xw[:, a, :] if mode == "weighted" else (X, X2)[h][:, a, :, :].rearrange("p s d -> p (s d)")
                                    first, last = a == 0 and h == 0, a == NT - 1 and h == H - 1
                                    if mode == "relation":
                                        pe.matmul(pR[0:64, 0:P], h3[:, q % NHB, k, :], h2[:, q % NHB, k, :], start=first, stop=last)
                                    mm = pe.matmul(pO[:, 0:width], Cs[:, u % 2, k, :], x, start=first, stop=last)
                                mm.then_inc(s_o, 1)
                            pe.wait_ge(s_o, (i + 1) * U + PRE)
                            pe.sem_inc(s_sum, 1)
                            if mode == "relation":
                                pe.wait_ge(s_rel, i + 1)
                                pe.matmul(pE[:, 0:P], rel_t[:, :], relw[:, :], start=True, stop=True).then_inc(s_relm, 1)

        def tiles_of(eng, g, destination):
            return nc.values_load_multi_w_load_instructions(
                tiles[0:1, bass.ds(g * PAIR, PAIR), (1 if destination else 0):(2 if destination else 1)].rearrange("a c b -> a (c b)"),
                engines=(eng.engine,), min_val=0, max_val=NT - 1, skip_runtime_bounds_check_because="records hold tiles below NT")[1]

        def aggregate_shared(mode, name):
            by_source = mode in ("relation", "typed")
            wide = 2 * P if by_source else P
            cdt = F32 if mode == "weighted" else BF16
            width = XW if mode == "weighted" else P
            NI = NOV // (2 * PAIR)
            NJ = max(d for d in range(1, 17) if NI % d == 0)
            with ExitStack() as c:
                h1 = sb(f"h1{name}", [P, 2, PAIR, 2 * P if mode == "typed" else P], cdt, c)
                h2 = sb(f"h2{name}", [P, 2, PAIR, P], cdt, c)
                h3 = sb(f"h3{name}", [P, 2, PAIR, 64], BF16, c) if mode == "relation" else None
                Cs = sb(f"Cs{name}", [P, 2, PAIR, wide], cdt, c)
                pC = [ps(f"pC{name}{i}", [P, PAIR, wide], c) for i in range(2)]
                pO = [ps(f"pO{name}{i}", [P, PAIR, 2 * P], c) for i in range(2)]
                iota = iota_f if mode == "weighted" else iota_b
                s_h1 = sem(f"s_h1{name}", c)
                s_c = sem(f"s_c{name}", c)
                s_cs = sem(f"s_cs{name}", c)
                s_o = sem(f"s_o{name}", c)
                s_acc = sem(f"s_acc{name}", c)

                with nc.Block() as block:
                    @block.vector
                    def _(v):
                        v.sem_inc(s_acc, 2 * PAIR)

                        def hot(g, par):
                            v.wait_ge(s_c, g + 1)

                            def same(o, f, w):
                                field = recs[:, bass.ds(BUCKETS + g * PAIR, PAIR), f] if f == F_SL else recs_h[:, bass.ds(BUCKETS + g * PAIR, PAIR), f]
                                return v.tensor_tensor(o, iota[:, 0:w].unsqueeze(1).broadcast_to([P, PAIR, w]),
                                                       field.unsqueeze(2).broadcast_to([P, PAIR, w]), ALU.is_equal)

                            same(h2[:, par, :, :], H_DL, P)
                            if mode == "relation":
                                same(h3[:, par, :, :], H_REL, 64)
                            if mode == "weighted":
                                for k in range(PAIR):
                                    f32 = recs[:, bass.ds(BUCKETS + g * PAIR + k, 1), F_SL:F_W + 1].rearrange("p a w -> p (a w)")
                                    ins = v.tensor_scalar(h1[:, par, k, :], iota[:, 0:P], f32[:, 0:1], f32[:, 1:2], ALU.is_equal, ALU.mult)
                            elif mode == "typed":
                                ins = same(h1[:, par, :, :], H_SL2, 2 * P)
                            else:
                                ins = same(h1[:, par, :, :], F_SL, P)
                            ins.then_inc(s_h1, 1)

                        count = v.value_load(n_over[0:1, 0:1], min_val=0, max_val=NOV)
                        with v.Fori(0, NI // NJ) as o:
                            with v.If(o * (NJ * 2 * PAIR) < count):
                                with v.Fori(0, NJ) as j:
                                    i = o * NJ + j
                                    with v.If(i * (2 * PAIR) < count):
                                        hot(2 * i, 0)
                                        hot(2 * i + 1, 1)
                                        for par in range(2):
                                            g = 2 * i + par
                                            bs = tiles_of(v, g, by_source)
                                            v.wait_ge(s_o, g + 3)
                                            for k in range(PAIR):
                                                v.wait_ge(s_acc, (g + 2) * PAIR + k)
                                                dst = acc[:, bass.ds(bs[k], 1), 0:width].rearrange("p a w -> p (a w)")
                                                v.tensor_tensor(dst, dst, pO[par][:, k, 0:width], ALU.add).then_inc(s_acc, 1)

                    @block.scalar
                    def _(act):
                        act.sem_inc(s_cs, DEPTH)

                        def evacuate(g, par):
                            act.wait_ge(s_c, g + 3)
                            act.wait_ge(s_o, g + 1)
                            if mode == "relation":
                                act.activation(Cs[:, par, :, 0:P], pC[par][:, :, 0:P], ACT.Copy)
                                act.activation(Cs[0:64, par, :, P:2 * P], pC[par][0:64, :, P:2 * P], ACT.Copy).then_inc(s_cs, 1)
                            else:
                                act.activation(Cs[:, par, :, :], pC[par][:, :, :], ACT.Copy).then_inc(s_cs, 1)

                        count = act.value_load(n_over[0:1, 0:1], min_val=0, max_val=NOV)
                        with act.Fori(0, NI // NJ) as o:
                            with act.If(o * (NJ * 2 * PAIR) < count):
                                with act.Fori(0, NJ) as j:
                                    i = o * NJ + j
                                    with act.If(i * (2 * PAIR) < count):
                                        for par in range(2):
                                            evacuate(2 * i + par, par)

                    @block.tensor
                    def _(pe):
                        pe.sem_inc(s_c, DEPTH)
                        pe.sem_inc(s_o, DEPTH)

                        def table(g, par):
                            pe.wait_ge(s_h1, g + 1)
                            pe.wait_ge(s_cs, g + 1)
                            for k in range(PAIR):
                                if by_source:
                                    mm = pe.matmul(pC[par][:, k, 0:P], h1[:, par, k, 0:P], h2[:, par, k, :], start=True, stop=True)
                                    if mode == "relation":
                                        mm = pe.matmul(pC[par][0:64, k, P:2 * P], h3[:, par, k, :], h2[:, par, k, :], start=True, stop=True)
                                    else:
                                        mm = pe.matmul(pC[par][:, k, P:2 * P], h1[:, par, k, P:2 * P], h2[:, par, k, :], start=True, stop=True)
                                else:
                                    mm = pe.matmul(pC[par][:, k, :], h2[:, par, k, :], h1[:, par, k, :], start=True, stop=True)
                            mm.then_inc(s_c, 1)

                        count = pe.value_load(n_over[0:1, 0:1], min_val=0, max_val=NOV)
                        with pe.Fori(0, NI // NJ) as o:
                            with pe.If(o * (NJ * 2 * PAIR) < count):
                                with pe.Fori(0, NJ) as j:
                                    i = o * NJ + j
                                    with pe.If(i * (2 * PAIR) < count):
                                        table(2 * i, 0)
                                        table(2 * i + 1, 1)
                                        for par in range(2):
                                            g = 2 * i + par
                                            As = tiles_of(pe, g, not by_source)
                                            pe.wait_ge(s_cs, g + 3)
                                            pe.wait_ge(s_acc, g * PAIR + PAIR)
                                            for k in range(PAIR):
                                                o = pO[par][:, k, 0:width]
                                                if mode == "weighted":
                                                    mm = pe.matmul(o, Cs[:, par, k, :], Xw[:, bass.ds(As[k], 1), :].rearrange("p a w -> p (a w)"), start=True, stop=True)
                                                else:
                                                    for s in range(3):
                                                        mm = pe.matmul(o, Cs[:, par, k, 0:P], X[:, bass.ds(As[k], 1), s, :].rearrange("p a w -> p (a w)"),
                                                                       start=(s == 0), stop=(s == 2 and not by_source))
                                                    if mode == "relation":
                                                        for s in range(3):
                                                            mm = pe.matmul(o, Cs[0:64, par, k, P:2 * P], relx[:, s, :], start=False, stop=(s == 2))
                                                    if mode == "typed":
                                                        for s in range(3):
                                                            mm = pe.matmul(o, Cs[:, par, k, P:2 * P], X2[:, bass.ds(As[k], 1), s, :].rearrange("p a w -> p (a w)"),
                                                                           start=False, stop=(s == 2))
                                            mm.then_inc(s_o, 1)

        X2 = None
        Xw = X[:, :, :, :].rearrange("p t s d -> p (t s d)").bitcast(F32)[:, 0:NT * XW].rearrange("p (t w) -> p t w", w=XW)
        G7 = max(d for d in range(1, 9) if NT % d == 0)
        WEIGHTS = [["L0_gnn_W_msg", "L0_gnn_W_self"], ["L1_gnn_W1", "L1_gnn_W0"],
                   ["L2_gnn_W_data", "L2_gnn_W_control", "L2_gnn_W_self"], ["L3_gnn_W"], []]
        VECTORS = [["L0_gnn_b_msg", "L0_gnn_b_self"], ["L1_gnn_b1", "L1_gnn_b0", "att", "scale1", "off1"],
                   ["L2_gnn_b_data", "L2_gnn_b_control", "L2_gnn_b_self", "scale0", "off0"], ["L3_gnn_b"], []]
        DV = P // HEADS

        def vector_of(name):
            if name == "att":
                return t["L1_gnn_attention"][1, :, :].rearrange("h d -> (h d)")
            if name[:-1] in ("scale", "off"):
                return t["L1_gnn_scale" if name[0] == "s" else "L1_gnn_offset"][int(name[-1]), :, :].rearrange("h d -> (h d)")
            return t[name]

        def node_stage(k):
            nW, nV = len(WEIGHTS[k]), len(VECTORS[k])
            with ExitStack() as c:
                WT = sb(f"WT{k}", [P, max(nW, 1), P], F32, c)
                vec = sb(f"vec{k}", [P, max(nV, 1), P], F32, c)
                W1 = sb(f"W1_{k}", [P, G7, P], F32, c)
                xT = sb(f"xT{k}", [P, G7, P], F32, c)
                st = sb(f"st{k}", [P, G7, 6], F32, c)
                mv = sb(f"mv{k}", [P, G7, 2], F32, c)
                sd = sb(f"sd{k}", [P, G7], F32, c)
                m4 = sb(f"m4_{k}", [P, G7, HEADS], F32, c)
                v4 = sb(f"v4_{k}", [P, G7, HEADS], F32, c)
                gm = sb(f"gm{k}", [P, 2, HEADS], F32, c)
                pT = ps(f"pT_{k}", [P, 8, P], c)
                pY = [ps(f"pY_{k}{j}", [P, 8, P], c) for j in range(3)]
                s_load, s_wt, s_wc = [sem(f"{n}{k}", c) if k < 4 else None for n in ("s_load", "s_wt", "s_wc")]
                s_rel = sem(f"s_rel{k}", c) if k == 0 else None
                s_link = sem(f"s_link{k}", c) if k == 0 else None
                s_ask = sem(f"s_ask{k}", c)
                s_sqrt = sem(f"s_sqrt{k}", c)
                s_new = sem(f"s_new{k}", c)
                s_tp, s_xt, s_y = [sem(f"{n}{k}", c) if k < 4 else None for n in ("s_tp", "s_xt", "s_y")]
                s_out = sem(f"s_out{k}", c) if k == 4 else None

                with nc.Block() as block:
                    @block.sync
                    def _(sp):
                        n = 0
                        for j, w in enumerate(WEIGHTS[k]):
                            sp.dma_start(W1[:, j, :], t[w]).then_inc(s_load, 16)
                            n += 16
                        for j, b in enumerate(VECTORS[k]):
                            sp.dma_start(vec[:, j, :], vector_of(b).rearrange("(a n) -> a n", a=1).broadcast_to([P, P])).then_inc(s_load, 16)
                            n += 16
                        if k == 0:
                            sp.dma_start(W1[0:REL, 3, :], t["L0_gnn_rel_emb"]).then_inc(s_load, 16)
                            full = N // P
                            sp.dma_start(B[:, 0:full, :], t["x"][0:full * P, :].rearrange("(t p) d -> p t d", p=P)).then_inc(s_load, 16)
                            sp.wait_ge(s_link, 1)
                            sp.dma_start(B[0:N - full * P, full, :], t["x"][full * P:N, :]).then_inc(s_load, 16)
                            n += 48
                        if n:
                            sp.wait_ge(s_load, n)

                    @block.tensor
                    def _(pe):
                        if nW:
                            pe.wait_ge(s_load, 16 * (nW + nV) + (48 if k == 0 else 0))
                            for j in range(nW):
                                pe.transpose(pT[:, j, :], W1[:, j, :], ident_f[:, :]).then_inc(s_wt, 1)
                        if k == 0:
                            pe.transpose(pT[:, 3, 0:REL], W1[0:REL, 3, :], ident_f[0:REL, 0:REL]).then_inc(s_wt, 1)
                            pe.wait_ge(s_wc, 2)
                            pe.matmul(pT[0:REL, 4, :], xT[:, 0, 0:REL], WT[:, 0, :], start=True, stop=True).then_inc(s_rel, 1)

                    @block.scalar
                    def _(act):
                        if nW:
                            act.wait_ge(s_wt, nW + (1 if k == 0 else 0))
                            act.activation(WT[:, :, :], pT[:, 0:nW, :], ACT.Copy).then_inc(s_wc, 1)
                        if k == 0:
                            act.activation(xT[:, 0, 0:REL], pT[:, 3, 0:REL], ACT.Copy).then_inc(s_wc, 1)

                    @block.vector
                    def _(v):
                        n = [0]

                        def link(ins):
                            n[0] += 1
                            ins.then_inc(s_link, 1)
                            v.wait_ge(s_link, n[0])

                        if k == 0:
                            link(v.memset(B[:, N // P, :], 0.0))
                            link(v.memset(acc[:, :, :], 0.0))
                            v.wait_ge(s_rel, 1)
                            link(v.tensor_copy(relw[:, :], pT[0:REL, 4, :]))
                            link(v.tensor_copy(relx[:, 0, :], pT[0:REL, 4, :]))
                            link(v.tensor_tensor(W1[0:REL, 4, :], pT[0:REL, 4, :], relx[:, 0, :], ALU.subtract))
                            link(v.tensor_copy(relx[:, 1, :], W1[0:REL, 4, :]))
                            link(v.tensor_tensor(relx[:, 2, :], W1[0:REL, 4, :], relx[:, 1, :], ALU.subtract))

                s_link2 = sem(f"s_link2{k}", c)

                def vector_steps(v, i, per, final):
                    n = [0]
                    asked = [0]
                    ROOTS = {0: 0, 1: 2, 2: 2, 3: 1, 4: 1}[k]

                    def link(ins):
                        n[0] += 1
                        ins.then_inc(s_link2, 1)
                        v.wait_ge(s_link2, i * per + n[0])

                    T = bass.ds(i * G7, G7)
                    Bt = B[:, T, :]
                    At = acc[:, T, 0:P]

                    def bc(ap, n3=P):
                        return ap.unsqueeze(2).broadcast_to([P, G7, n3])

                    def heads(ap):
                        return ap.rearrange("p t (h d) -> p t h d", h=HEADS)

                    def bch(ap):
                        return ap.unsqueeze(3).broadcast_to([P, G7, HEADS, DV])

                    def bv(j):
                        return vec[:, j, :].unsqueeze(1).broadcast_to([P, G7, P])

                    def root():
                        asked[0] += 1
                        v.wait_ge(s_sqrt, i * ROOTS + asked[0])

                    def norm_heads(src):
                        apart(v)
                        link(v.tensor_reduce(m4[:, :, :], heads(src), AX.X, ALU.add))
                        link(v.tensor_scalar(m4[:, :, :], m4[:, :, :], 1.0 / DV, None, ALU.mult))
                        link(v.tensor_tensor(heads(W1[:, :, :]), heads(src), bch(m4[:, :, :]), ALU.subtract))
                        link(v.tensor_tensor(xT[:, :, :], W1[:, :, :], W1[:, :, :], ALU.mult))
                        link(v.tensor_reduce(v4[:, :, :], heads(xT[:, :, :]), AX.X, ALU.add))
                        v.tensor_scalar(v4[:, :, :], v4[:, :, :], 1.0 / DV, 1e-9, ALU.mult, ALU.add).then_inc(s_ask, 1)
                        root()
                        link(v.reciprocal(m4[:, :, :], v4[:, :, :]))
                        link(v.tensor_tensor(heads(W1[:, :, :]), heads(W1[:, :, :]), bch(m4[:, :, :]), ALU.mult))

                    def split(dst, y):
                        link(v.tensor_scalar(dst[:, T, 0, :], y, 1.0, None, ALU.mult))
                        link(v.tensor_tensor(y, y, dst[:, T, 0, :], ALU.subtract))
                        link(v.tensor_scalar(dst[:, T, 1, :], y, 1.0, None, ALU.mult))
                        link(v.tensor_tensor(dst[:, T, 2, :], y, dst[:, T, 1, :], ALU.subtract))

                    if k == 1:
                        link(v.tensor_tensor(At, At, bc(deg_in[:, T]), ALU.mult))
                        link(v.tensor_tensor(Bt, Bt, At, ALU.add))
                    if k == 2:
                        link(v.tensor_scalar(v4[:, :, :], acc[:, T, P:XW], 1e-30, None, ALU.max))
                        link(v.reciprocal(v4[:, :, :], v4[:, :, :]))
                        link(v.tensor_tensor(heads(At), heads(At), bch(v4[:, :, :]), ALU.mult))
                        norm_heads(At)
                        link(v.tensor_tensor(W1[:, :, :], W1[:, :, :], bv(3), ALU.mult))
                        link(v.tensor_tensor(W1[:, :, :], W1[:, :, :], bv(4), ALU.add))
                        link(v.scalar_tensor_tensor(out=Bt, in0=W1[:, :, :], scalar=0.5, in1=Bt, op0=ALU.mult, op1=ALU.add))
                    if k == 3:
                        link(v.tensor_scalar(At, At, 0.0, None, ALU.max))
                        link(v.tensor_tensor(Bt, Bt, At, ALU.add))
                    if k == 4:
                        link(v.tensor_tensor(At, At, bc(deg_out[:, T]), ALU.mult))
                        link(v.tensor_tensor(Bt, Bt, At, ALU.add))
                    if k > 0:
                        apart(v)
                        for j in range(G7):
                            ins = v.bn_stats(st[:, j, :], B[:, bass.ds(i * G7 + j, 1), :].rearrange("p a d -> p (a d)"))
                        link(ins)
                        apart(v)
                        for j in range(G7):
                            ins = v.bn_aggr(mv[:, j, :], st[:, j, :])
                        ins.then_inc(s_ask, 1)
                        root()
                        link(v.reciprocal(sd[:, :], sd[:, :]))
                        link(v.tensor_tensor(Bt, Bt, mv[:, :, 0:1].broadcast_to([P, G7, P]), ALU.subtract))
                        link(v.tensor_tensor(Bt, Bt, bc(sd[:, :]), ALU.mult))
                    if k < 4:
                        link(v.tensor_scalar(W1[:, :, :], Bt, 1.0, None, ALU.mult))
                    v.sem_inc(s_new, 1)
                    if k == 4:
                        return n[0]
                    v.wait_ge(s_y, i + 1)
                    Y = [p[:, 0:G7, :] for p in pY]
                    y = W1[:, :, :]
                    if k == 0:
                        link(v.tensor_tensor(y, Y[0], bv(0), ALU.add))
                        split(X, y)
                        link(v.tensor_tensor(Bt, Bt, Y[1], ALU.add))
                        link(v.tensor_tensor(Bt, Bt, bv(1), ALU.add))
                    if k == 1:
                        link(v.tensor_tensor(y, Y[0], bv(0), ALU.add))
                        link(v.tensor_scalar(Xw[:, T, 0:P], y, 0.0, None, ALU.max))
                        link(v.tensor_tensor(y, Xw[:, T, 0:P], bv(2), ALU.mult))
                        link(v.tensor_reduce(m4[:, :, :], heads(y), AX.X, ALU.add))
                        link(v.scalar_tensor_tensor(out=Xw[:, T, P:XW], in0=m4[:, :, :], scalar=0.2, in1=m4[:, :, :], op0=ALU.mult, op1=ALU.max))
                        link(v.tensor_tensor(y, Y[1], bv(1), ALU.add))
                        link(v.tensor_scalar(y, y, 0.0, None, ALU.max))
                        norm_heads(y)
                        link(v.tensor_tensor(y, y, bv(3), ALU.mult))
                        link(v.tensor_tensor(y, y, bv(4), ALU.add))
                        link(v.scalar_tensor_tensor(out=Bt, in0=y, scalar=0.5, in1=Bt, op0=ALU.mult, op1=ALU.add))
                    if k == 2:
                        link(v.tensor_tensor(y, Y[0], bv(0), ALU.add))
                        split(X, y)
                        link(v.tensor_tensor(y, Y[1], bv(1), ALU.add))
                        split(X2, y)
                        link(v.tensor_tensor(At, Y[2], bv(2), ALU.add))
                    if k == 3:
                        link(v.tensor_tensor(y, Y[0], bv(0), ALU.add))
                        link(v.tensor_tensor(y, y, bc(deg_out[:, T]), ALU.mult))
                        link(v.tensor_scalar(At, y, 1.0, None, ALU.mult))
                        split(X, y)
                    return n[0]

                PER = {0: 8, 1: 24, 2: 29, 3: 14, 4: 6}[k]
                ROOTS = {0: 0, 1: 2, 2: 2, 3: 1, 4: 1}[k]
                NB = NT // G7

                with nc.Block() as block:
                    @block.vector
                    def _(v):
                        with v.Fori(0, NB) as i:
                            n = vector_steps(v, i, PER, False)
                        assert n == PER, (k, n)

                    @block.scalar
                    def _(act):
                        with act.Fori(0, NB) as i:
                            def root(r, which):
                                act.wait_ge(s_ask, i * ROOTS + r)
                                if which == "norm":
                                    act.activation(sd[:, :], mv[:, :, 1:2].rearrange("p t a -> p (t a)"), ACT.Sqrt, bias=eps[:, 0:1]).then_inc(s_sqrt, 1)
                                else:
                                    act.activation(v4[:, :, :], v4[:, :, :], ACT.Sqrt).then_inc(s_sqrt, 1)

                            if k == 2:
                                root(1, "heads")
                            if k > 0:
                                root(2 if k == 2 else 1, "norm")
                            if k < 4:
                                act.wait_ge(s_tp, i + 1)
                                act.activation(xT[:, :, :], pT[:, 0:G7, :], ACT.Copy).then_inc(s_xt, 1)
                            if k == 1:
                                root(2, "heads")

                    @block.tensor
                    def _(pe):
                        if k == 4:
                            return
                        with pe.Fori(0, NB) as i:
                            pe.wait_ge(s_new, i + 1)
                            for j in range(G7):
                                tr = pe.transpose(pT[:, j, :], W1[:, j, :], ident_f[:, :])
                            tr.then_inc(s_tp, 1)
                            pe.wait_ge(s_xt, i + 1)
                            for w in range(nW):
                                for j in range(G7):
                                    mm = pe.matmul(pY[w][:, j, :], xT[:, j, :], WT[:, w, :], start=True, stop=True)
                            mm.then_inc(s_y, 1)

                    @block.sync
                    def _(sp):
                        if k == 4:
                            full = N // P
                            sp.wait_ge(s_new, NB)
                            sp.dma_start(out[0:full * P, :].rearrange("(t p) d -> p t d", p=P), B[:, 0:full, :]).then_inc(s_out, 16)
                            sp.dma_start(out[full * P:N, :], B[0:N - full * P, full, :]).then_inc(s_out, 16)
                            sp.wait_ge(s_out, 32)

                if k == 1:
                    s_gm = sem("s_gm", c)
                    s_gp = sem("s_gp", c)
                    s_e = sem("s_e", c)
                    s_ex = sem("s_ex", c)
                    q = Xw[:, :, P:XW]
                    with nc.Block() as block:
                        @block.vector
                        def _(v):
                            v.memset(acc[:, :, :], 0.0)
                            v.tensor_reduce(gm[:, 0, :], q.rearrange("p t h -> p h t"), AX.X, ALU.max).then_inc(s_gm, 1)
                            v.wait_ge(s_gp, 1)
                            v.tensor_tensor(q, q, gm[:, 1, :].unsqueeze(1).broadcast_to([P, NT, HEADS]), ALU.subtract).then_inc(s_e, 1)
                            v.wait_ge(s_ex, 1)
                            h = Xw[:, :, 0:P].rearrange("p t (h d) -> p t h d", h=HEADS)
                            v.tensor_tensor(h, h, q.unsqueeze(3).broadcast_to([P, NT, HEADS, DV]), ALU.mult).then_inc(s_e, 1)

                        @block.gpsimd
                        def _(gp):
                            gp.wait_ge(s_gm, 1)
                            gp.partition_all_reduce(gm[:, 1, :], gm[:, 0, :], P, RMAX).then_inc(s_gp, 1)

                        @block.scalar
                        def _(act):
                            act.wait_ge(s_e, 1)
                            act.activation(q, q, ACT.Exp).then_inc(s_ex, 1)

        node_stage(0)
        aggregate_own("relation", "0")
        aggregate_shared("relation", "0")
        node_stage(1)
        aggregate_own("weighted", "1")
        aggregate_shared("weighted", "1")
        X2 = sb("X2", [P, NT, 3, P], BF16)
        node_stage(2)
        aggregate_own("typed", "2")
        aggregate_shared("typed", "2")
        node_stage(3)
        aggregate_own("plain", "3")
        aggregate_shared("plain", "3")
        node_stage(4)


_INS = ["x", "src", "dst", "edge_type_2", "edge_type_64", "edge_weight",
        "L0_gnn_W_self", "L0_gnn_b_self", "L0_gnn_W_msg", "L0_gnn_b_msg", "L0_gnn_rel_emb",
        "L1_gnn_W0", "L1_gnn_b0", "L1_gnn_W1", "L1_gnn_b1", "L1_gnn_attention", "L1_gnn_scale", "L1_gnn_offset",
        "L2_gnn_W_data", "L2_gnn_b_data", "L2_gnn_W_control", "L2_gnn_b_control", "L2_gnn_W_self", "L2_gnn_b_self",
        "L3_gnn_W", "L3_gnn_b"]


def kernel(**inputs):
    import numpy as _np
    import concourse.bacc as _bacc
    from concourse import mybir as _mybir
    from concourse.bass_utils import run_bass_kernel_spmd as _run

    nc = _bacc.Bacc("TRN2", target_bir_lowering=False, num_devices=1)
    arrays, args = {}, {}
    for name in _INS:
        a = _np.ascontiguousarray(inputs[name])
        arrays[f"in_{name}"] = a
        args[name] = nc.dram_tensor(f"in_{name}", a.shape, _mybir.dt.from_np(a.dtype), kind="ExternalInput").ap()
    out = nc.dram_tensor("out_0", inputs["x"].shape, _mybir.dt.float32, kind="ExternalOutput").ap()
    gnn_four_layers_kernel(nc, args, out)
    r = _run(nc, [arrays], core_ids=[0])
    return r.results[0]["out_0"]
```
